# Optimizing a Trainium2 kernel written in Bass

```python
import numpy as np
import jax
import jax.numpy as jnp

def _softmax(x, axis=-1):
    return jax.nn.softmax(x, axis=axis)

def _gelu(x):
    return jax.nn.gelu(x, approximate=True)

def _silu(x):
    return jax.nn.silu(x)

def _sigmoid(x):
    return jax.nn.sigmoid(x)

def _layernorm(x, axis=-1, eps=1e-05):
    m = jnp.mean(x, axis=axis, keepdims=True)
    v = jnp.var(x, axis=axis, keepdims=True)
    return (x - m) / jnp.sqrt(v + eps)

def _scatter_add(tgt, idx, src, axis=0):
    return tgt.at[idx].add(src)

def _segment_sum(src, seg, n):
    return jax.ops.segment_sum(src, seg, n)
kernel_name = 'mk_prb_d2_jaxref_r8_9c1601'

def setup_inputs(seed: int=0):
    np.random.seed(seed)
    _w = jnp.asarray

    def _L0_attn_setup():
        import jax, jax.numpy as jnp
        import numpy as np
        HID = 256
        HEADS = 16
        HD = HID // HEADS
        EPS = 1e-06

        def _heads(x, b, s):
            return x.reshape(b, s, HEADS, HD).transpose(0, 2, 1, 3)
        key = jax.random.key(seed)
        ks = jax.random.split(key, 9)
        s = 1.0 / np.sqrt(HID)
        return {'hidden_states': jax.random.normal(ks[0], (4, 512, HID), jnp.float32), 'q_w': jax.random.normal(ks[1], (HID, HID), jnp.float32) * s, 'q_b': jnp.zeros((HID,), jnp.float32), 'k_w': jax.random.normal(ks[2], (HID, HID), jnp.float32) * s, 'k_b': jnp.zeros((HID,), jnp.float32), 'v_w': jax.random.normal(ks[3], (HID, HID), jnp.float32) * s, 'v_b': jnp.zeros((HID,), jnp.float32), 'o_w': jax.random.normal(ks[4], (HID, HID), jnp.float32) * s, 'o_b': jnp.zeros((HID,), jnp.float32)}
    _L0_attn_in = _L0_attn_setup()

    def _L0_ffn_setup():
        import jax, jax.numpy as jnp
        import numpy as np
        D_MODEL = 256
        D_EXPERT = 1024
        EPS = 1e-08

        def ternary_quant(w):
            scale = jnp.mean(jnp.abs(w)) + EPS
            q = jnp.clip(jnp.round(w / scale), -1.0, 1.0) * scale
            return w + jax.lax.stop_gradient(q - w)
        key = jax.random.key(seed)
        k_x, k_up, k_gate, k_down = jax.random.split(key, 4)
        std_in = 1.0 / np.sqrt(D_MODEL)
        std_exp = 1.0 / np.sqrt(D_EXPERT)
        return {'x': jax.random.normal(k_x, (4, 256, D_MODEL), dtype=jnp.float32), 'W_up': jax.random.normal(k_up, (D_EXPERT, D_MODEL), dtype=jnp.float32) * std_in, 'W_gate': jax.random.normal(k_gate, (D_EXPERT, D_MODEL), dtype=jnp.float32) * std_in, 'W_down': jax.random.normal(k_down, (D_MODEL, D_EXPERT), dtype=jnp.float32) * std_exp}
    _L0_ffn_in = _L0_ffn_setup()

    def _L1_attn_setup():
        import jax, jax.numpy as jnp
        import numpy as np
        EMBED_DIM = 256
        NUM_HEADS = 16
        HEAD_DIM = EMBED_DIM // NUM_HEADS
        BASE = 10000.0

        def rotate_half(x):
            half = x.shape[-1] // 2
            x1, x2 = (x[..., :half], x[..., half:])
            return jnp.concatenate([-x2, x1], axis=-1)

        def apply_rope(x, base=BASE):
            S, Dh = (x.shape[-2], x.shape[-1])
            inv_freq = 1.0 / base ** (jnp.arange(0, Dh, 2, dtype=jnp.float32) / Dh)
            t = jnp.arange(S, dtype=jnp.float32)
            freqs = jnp.einsum('i,j->ij', t, inv_freq)
            emb = jnp.concatenate([freqs, freqs], axis=-1)
            return x * jnp.cos(emb) + rotate_half(x) * jnp.sin(emb)
        key = jax.random.key(seed)
        ks = jax.random.split(key, 9)
        B, S, D = (2, 256, EMBED_DIM)
        xavier = lambda k, shape: jax.random.uniform(k, shape, jnp.float32, -1.0, 1.0) * float(np.sqrt(6.0 / (shape[0] + shape[1])))
        return {'x': jax.random.normal(ks[0], (B, S, D), jnp.float32), 'q_w': xavier(ks[1], (D, D)), 'k_w': xavier(ks[2], (D, D)), 'v_w': xavier(ks[3], (D, D)), 'q_b': jnp.zeros((D,), jnp.float32), 'k_b': jnp.zeros((D,), jnp.float32), 'v_b': jnp.zeros((D,), jnp.float32), 'out_w': xavier(ks[4], (D, D)), 'out_b': jnp.zeros((D,), jnp.float32)}
    _L1_attn_in = _L1_attn_setup()

    def _L1_ffn_setup():
        import jax, jax.numpy as jnp
        import numpy as np
        HIDDEN = 256
        INTER = 1024
        SCALE = 64.0

        def fwht(x):
            orig_shape = x.shape
            n = orig_shape[-1]
            x = x.reshape(-1, n)
            h = 1
            while h < n:
                x = x.reshape(-1, n // (2 * h), 2, h)
                a, b = (x[:, :, 0, :], x[:, :, 1, :])
                x = jnp.stack([a + b, a - b], axis=2).reshape(-1, n)
                h *= 2
            return (x / jnp.sqrt(jnp.asarray(n, x.dtype))).reshape(orig_shape)
        key = jax.random.key(seed)
        ks = jax.random.split(key, 8)
        inp = jax.random.normal(ks[0], (4, 256, HIDDEN), dtype=jnp.float32)
        SU_ug = jnp.where(jax.random.bernoulli(ks[1], 0.5, (HIDDEN,)), 1.0, -1.0).astype(jnp.float32)
        SU_dp = jnp.where(jax.random.bernoulli(ks[2], 0.5, (INTER,)), 1.0, -1.0).astype(jnp.float32)
        Wscale_ug = jax.random.uniform(ks[3], (2 * INTER,), jnp.float32, 0.5, 1.5)
        Wscale_dp = jax.random.uniform(ks[4], (HIDDEN,), jnp.float32, 0.5, 1.5)
        W_up = jax.random.normal(ks[5], (INTER, HIDDEN), dtype=jnp.float32) * 0.02
        W_gate = jax.random.normal(ks[6], (INTER, HIDDEN), dtype=jnp.float32) * 0.02
        W_down = jax.random.normal(ks[7], (HIDDEN, INTER), dtype=jnp.float32) * 0.02
        return {'input': inp, 'SU_ug': SU_ug, 'SU_dp': SU_dp, 'Wscale_ug': Wscale_ug, 'Wscale_dp': Wscale_dp, 'W_up': W_up, 'W_gate': W_gate, 'W_down': W_down}
    _L1_ffn_in = _L1_ffn_setup()
    _d = {'L0_attn_hidden_states': _L0_attn_in['hidden_states'], 'L0_attn_q_w': _L0_attn_in['q_w'], 'L0_attn_q_b': _L0_attn_in['q_b'], 'L0_attn_k_w': _L0_attn_in['k_w'], 'L0_attn_k_b': _L0_attn_in['k_b'], 'L0_attn_v_w': _L0_attn_in['v_w'], 'L0_attn_v_b': _L0_attn_in['v_b'], 'L0_attn_o_w': _L0_attn_in['o_w'], 'L0_attn_o_b': _L0_attn_in['o_b'], 'L0_ffn_W_up': _L0_ffn_in['W_up'], 'L0_ffn_W_gate': _L0_ffn_in['W_gate'], 'L0_ffn_W_down': _L0_ffn_in['W_down'], 'L1_attn_q_w': _L1_attn_in['q_w'], 'L1_attn_k_w': _L1_attn_in['k_w'], 'L1_attn_v_w': _L1_attn_in['v_w'], 'L1_attn_q_b': _L1_attn_in['q_b'], 'L1_attn_k_b': _L1_attn_in['k_b'], 'L1_attn_v_b': _L1_attn_in['v_b'], 'L1_attn_out_w': _L1_attn_in['out_w'], 'L1_attn_out_b': _L1_attn_in['out_b'], 'L1_ffn_SU_ug': _L1_ffn_in['SU_ug'], 'L1_ffn_SU_dp': _L1_ffn_in['SU_dp'], 'L1_ffn_Wscale_ug': _L1_ffn_in['Wscale_ug'], 'L1_ffn_Wscale_dp': _L1_ffn_in['Wscale_dp'], 'L1_ffn_W_up': _L1_ffn_in['W_up'], 'L1_ffn_W_gate': _L1_ffn_in['W_gate'], 'L1_ffn_W_down': _L1_ffn_in['W_down']}
    _x0 = _d['L0_attn_hidden_states']
    _d['L0_attn_hidden_states'] = jax.random.normal(jax.random.fold_in(jax.random.key(seed), 1), (2, 1024, 256), dtype=_x0.dtype)
    del _x0
    return _d

def reference(L0_attn_hidden_states, L0_attn_q_w, L0_attn_q_b, L0_attn_k_w, L0_attn_k_b, L0_attn_v_w, L0_attn_v_b, L0_attn_o_w, L0_attn_o_b, L0_ffn_W_up, L0_ffn_W_gate, L0_ffn_W_down, L1_attn_q_w, L1_attn_k_w, L1_attn_v_w, L1_attn_q_b, L1_attn_k_b, L1_attn_v_b, L1_attn_out_w, L1_attn_out_b, L1_ffn_SU_ug, L1_ffn_SU_dp, L1_ffn_Wscale_ug, L1_ffn_Wscale_dp, L1_ffn_W_up, L1_ffn_W_gate, L1_ffn_W_down):

    def _L0_attn_ref(hidden_states, q_w, q_b, k_w, k_b, v_w, v_b, o_w, o_b):
        import jax, jax.numpy as jnp
        import numpy as np
        HID = 256
        HEADS = 16
        HD = HID // HEADS
        EPS = 1e-06

        def _heads(x, b, s):
            return x.reshape(b, s, HEADS, HD).transpose(0, 2, 1, 3)
        b, s, _ = hidden_states.shape
        q = _heads(hidden_states @ q_w.T + q_b, b, s)
        k = _heads(hidden_states @ k_w.T + k_b, b, s)
        v = _heads(hidden_states @ v_w.T + v_b, b, s)
        qp = jax.nn.elu(q) + 1.0
        kp = jax.nn.elu(k) + 1.0
        kv = jnp.einsum('bhsd,bhse->bhde', kp, v)
        z = jnp.einsum('bhsd,bhd->bhs', qp, kp.sum(axis=2))[..., None]
        attn = jnp.einsum('bhsd,bhde->bhse', qp, kv) / (z + EPS)
        out = attn.transpose(0, 2, 1, 3).reshape(b, s, HID)
        return out @ o_w.T + o_b

    def _L0_ffn_ref(x, W_up, W_gate, W_down):
        import jax, jax.numpy as jnp
        import numpy as np
        D_MODEL = 256
        D_EXPERT = 1024
        EPS = 1e-08

        def ternary_quant(w):
            scale = jnp.mean(jnp.abs(w)) + EPS
            q = jnp.clip(jnp.round(w / scale), -1.0, 1.0) * scale
            return w + jax.lax.stop_gradient(q - w)
        wu = ternary_quant(W_up)
        wg = ternary_quant(W_gate)
        wd = ternary_quant(W_down)
        up = jnp.einsum('bsd,ed->bse', x, wu)
        gate = jnp.einsum('bsd,ed->bse', x, wg)
        hidden = jax.nn.silu(up) * gate
        return jnp.einsum('bse,de->bsd', hidden, wd)

    def _L1_attn_ref(x, q_w, k_w, v_w, q_b, k_b, v_b, out_w, out_b):
        import jax, jax.numpy as jnp
        import numpy as np
        EMBED_DIM = 256
        NUM_HEADS = 16
        HEAD_DIM = EMBED_DIM // NUM_HEADS
        BASE = 10000.0

        def rotate_half(x):
            half = x.shape[-1] // 2
            x1, x2 = (x[..., :half], x[..., half:])
            return jnp.concatenate([-x2, x1], axis=-1)

        def apply_rope(x, base=BASE):
            S, Dh = (x.shape[-2], x.shape[-1])
            inv_freq = 1.0 / base ** (jnp.arange(0, Dh, 2, dtype=jnp.float32) / Dh)
            t = jnp.arange(S, dtype=jnp.float32)
            freqs = jnp.einsum('i,j->ij', t, inv_freq)
            emb = jnp.concatenate([freqs, freqs], axis=-1)
            return x * jnp.cos(emb) + rotate_half(x) * jnp.sin(emb)
        B, S, D = x.shape
        H, Dh = (NUM_HEADS, HEAD_DIM)
        scaling = Dh ** (-0.5)
        q = (x @ q_w.T + q_b).reshape(B, S, H, Dh).transpose(0, 2, 1, 3)
        k = (x @ k_w.T + k_b).reshape(B, S, H, Dh).transpose(0, 2, 1, 3)
        v = (x @ v_w.T + v_b).reshape(B, S, H, Dh).transpose(0, 2, 1, 3)
        q = apply_rope(q)
        k = apply_rope(k)
        attn = jnp.einsum('bhqd,bhkd->bhqk', q, k) * scaling
        probs = jax.nn.softmax(attn, axis=-1)
        out = jnp.einsum('bhqk,bhkd->bhqd', probs, v)
        out = out.transpose(0, 2, 1, 3).reshape(B, S, D)
        return out @ out_w.T + out_b

    def _L1_ffn_ref(input, SU_ug, SU_dp, Wscale_ug, Wscale_dp, W_up, W_gate, W_down):
        import jax, jax.numpy as jnp
        import numpy as np
        HIDDEN = 256
        INTER = 1024
        SCALE = 64.0

        def fwht(x):
            orig_shape = x.shape
            n = orig_shape[-1]
            x = x.reshape(-1, n)
            h = 1
            while h < n:
                x = x.reshape(-1, n // (2 * h), 2, h)
                a, b = (x[:, :, 0, :], x[:, :, 1, :])
                x = jnp.stack([a + b, a - b], axis=2).reshape(-1, n)
                h *= 2
            return (x / jnp.sqrt(jnp.asarray(n, x.dtype))).reshape(orig_shape)
        n = SU_ug.shape[0]
        x = input.reshape(-1, n)
        x = fwht(x * SU_ug) / SCALE
        x_up = x @ W_up.T * (Wscale_ug[:INTER] * SCALE)
        x_gate = x @ W_gate.T * (Wscale_ug[INTER:] * SCALE)
        x = jax.nn.silu(x_gate) * x_up
        x = fwht(x * SU_dp) / SCALE
        x = x @ W_down.T * (Wscale_dp * SCALE)
        return x.reshape(input.shape)
    x = L0_attn_hidden_states
    xn = _layernorm(x, axis=-1)
    x = x + _L0_attn_ref(xn, L0_attn_q_w, L0_attn_q_b, L0_attn_k_w, L0_attn_k_b, L0_attn_v_w, L0_attn_v_b, L0_attn_o_w, L0_attn_o_b) + _L0_ffn_ref(xn, L0_ffn_W_up, L0_ffn_W_gate, L0_ffn_W_down)
    xn = _layernorm(x, axis=-1)
    x = x + _L1_attn_ref(xn, L1_attn_q_w, L1_attn_k_w, L1_attn_v_w, L1_attn_q_b, L1_attn_k_b, L1_attn_v_b, L1_attn_out_w, L1_attn_out_b) + _L1_ffn_ref(xn, L1_ffn_SU_ug, L1_ffn_SU_dp, L1_ffn_Wscale_ug, L1_ffn_Wscale_dp, L1_ffn_W_up, L1_ffn_W_gate, L1_ffn_W_down)
    return x

_drawn_inputs = setup_inputs


def setup_inputs(seed=0):
    import zlib

    import numpy as np

    out = dict(_drawn_inputs(seed))
    spreads = {'L0_attn_q_b': (0.0, 2.0),
     'L0_attn_k_b': (0.0, 2.0),
     'L0_attn_v_b': (0.0, 0.1),
     'L0_attn_o_b': (0.0, 0.1),
     'L1_attn_q_b': (0.0, 2.0),
     'L1_attn_k_b': (0.0, 2.0),
     'L1_attn_v_b': (0.0, 0.378),
     'L1_attn_out_b': (0.0, 0.405)}
    factors = {'L0_attn_q_w': 7.63,
     'L0_attn_k_w': 3.182,
     'L1_ffn_Wscale_ug': 4.163,
     'L1_ffn_Wscale_dp': 5.791}
    for name, (base, spread) in spreads.items():
        noise = np.random.default_rng([zlib.crc32(name.encode()), seed]).standard_normal(out[name].shape)
        drawn = base * np.exp(spread * noise) if base else spread * noise
        out[name] = jnp.asarray(drawn.astype(out[name].dtype))
    for name, factor in factors.items():
        out[name] = (out[name] * factor).astype(out[name].dtype)
    return out
```

```python
from contextlib import ExitStack

import concourse.bass as bass
from concourse import mybir

F32 = mybir.dt.float32
F32R = mybir.dt.float32r
ALU = mybir.AluOpType
ACT = mybir.ActivationFunctionType
AX = mybir.AxisListType

NT = 2048
NCH = 4
KB = 1024

COLS = dict(qb0=(0, 2), ob0=(2, 2), qb1=(4, 2), qsb1=(6, 2), kb1=(8, 2), ksb1=(10, 2), vb1=(12, 2), ob1=(14, 2),
            suu=(16, 2), sud=(18, 8), wsu=(26, 8), wsg=(34, 8), wsd=(42, 2), rowa=(44, 1), rowb=(45, 1), eps=(46, 1), eps5=(47, 1))
NCOL = 48


class Queue:

    def __init__(self, sem):
        self.sem, self.n, self.ops, self.seen = sem, 0, [], {}

    def wait(self, *tokens):
        for t in tokens:
            if t is None:
                continue
            sem, v = t
            if self.seen.get(sem.name, 0) < v:
                self.seen[sem.name] = v
                self.ops.append(lambda e, sem=sem, v=v: e.wait_ge(sem, v))

    def do(self, f, *tokens):
        self.wait(*tokens)
        self.n += 1
        self.ops.append(lambda e: f(e).then_inc(self.sem, 1))
        return self.sem, self.n

    def put(self, f, *tokens):
        self.wait(*tokens)
        self.ops.append(f)

    def last(self):
        return (self.sem, self.n) if self.n else None

    def run(self, e):
        for f in self.ops:
            f(e)


class Arrivals:

    def __init__(self, sem):
        self.sem, self.n = sem, 0

    def start(self, q, out, in_, *tokens):
        self.n += 16
        out, in_ = (a.bitcast(F32) if a.dtype == F32R else a for a in (out, in_))
        q.put(lambda e: e.dma_start(out, in_).then_inc(self.sem, 16), *tokens)
        return self.sem, self.n


class Ring:

    def __init__(self, slots):
        self.slots, self.free, self.i = slots, [None] * len(slots), -1

    def next(self):
        self.i = (self.i + 1) % len(self.slots)
        return self.slots[self.i], self.free[self.i], self.i


def program(nc, xT, wa0, tern, wa1, wo1, wf1, cols_d, bkv_d, cos_d, sin_d, had_d, mask_d, ident_d, yT):
    with ExitStack() as ctx:
        def sem(name):
            return ctx.enter_context(nc.semaphore(name))

        base = -(-nc.sbuf_base // 32) * 32

        def sb(name, kb, shape, dt=F32):
            return nc.alloc_sbuf_tensor_at(name, shape, dt, offset=base + int(kb * KB))

        V, A, G, T, S = (Queue(sem(n)) for n in ("s_dve", "s_act", "s_pool", "s_pe", "s_sp"))

        def dsem(name):
            return Arrivals(sem(name))

        X = sb("X", 0, [128, 2, NT])
        COS = sb("COS", 16, [128, 1024])
        SIN = sb("SIN", 20, [128, 1024])
        cols = sb("cols", 24, [128, NCOL])
        s16 = sb("s16", 24.25, [128, 16])
        HAD = sb("HAD", 24.5, [128, 128])
        HADN = sb("HADN", 25, [128, 128])
        IDN = sb("IDN", 25.5, [128, 128])
        MASK = sb("MASK", 26, [128, 128])
        MEAN = sb("MEAN", 26.5, [128, 128])
        ONES = sb("ONES", 27, [128, 128])
        mx = [sb(f"mx{i}", 27.5 + i / 16, [128, 16]) for i in range(2)]
        mrow = [sb(f"mrow{i}", 206 + i / 2, [16, 128], F32R) for i in range(2)]
        XH = sb("XH", 28, [128, 2, NT], F32R)
        XL = sb("XL", 44, [128, 2, NT], F32R)
        W0H = sb("W0H", 60, [128, 2, 1024], F32R)
        W0L = sb("W0L", 68, [128, 2, 1024], F32R)
        W1H = sb("W1H", 60, [128, 2, 1280], F32R)
        W1L = sb("W1L", 70, [128, 2, 1280], F32R)
        WOH = sb("WOH", 80, [128, 2, 256], F32R)
        WOL = sb("WOL", 82, [128, 2, 256], F32R)
        TU = sb("TU", 84, [128, 2, 1024], F32R)
        TG = sb("TG", 92, [128, 2, 1024], F32R)
        TD = sb("TD", 100, [128, 8, 256], F32R)
        QP = sb("QP", 108, [128, 2, NT])
        zk = [sb(f"zk{i}", 124 + i, [128, 256]) for i in range(2)]
        ek = [sb(f"ek{i}", 126 + i, [128, 256]) for i in range(2)]
        rk = [sb(f"rk{i}", 128 + i, [128, 256]) for i in range(2)]
        kp = [sb(f"kp{i}", 130 + i, [128, 256]) for i in range(2)]
        ve = [sb(f"ve{i}", 132 + 1.25 * i, [128, 2, 129]) for i in range(2)]
        kvb = [sb(f"kvb{i}", 135 + i / 2, [128, 128]) for i in range(2)]
        zb = [sb(f"zb{i}", 136 + i / 2, [128, 128]) for i in range(2)]
        zs = [sb(f"zs{i}", 137 + 2 * i, [128, 512]) for i in range(2)]
        at = [sb(f"at{i}", 141 + 4 * i, [128, 2, 512]) for i in range(1)][0]
        AH = sb("AH", 145, [128, 2, 512], F32R)
        AL = sb("AL", 149, [128, 2, 512], F32R)
        BKV = sb("BKV", 153, [128, 512])
        UGH = sb("UGH", 108, [128, 2, 2048], F32R)
        UGL = sb("UGL", 124, [128, 2, 2048], F32R)
        DH = sb("DH", 140, [128, 8, 256], F32R)
        DL = sb("DL", 148, [128, 8, 256], F32R)
        hh = [sb(f"hh{i}", 156 + 2 * i, [128, 512], F32R) for i in range(3)]
        hl = [sb(f"hl{i}", 162 + 2 * i, [128, 512], F32R) for i in range(3)]
        sg = [sb(f"sg{i}", 168 + 2 * i, [128, 512]) for i in range(3)]
        stg = [sb(f"stg{i}", 174 + 8 * i, [128, 2048]) for i in range(2)]
        XC = [sb(f"XC{i}", 190 + 4 * i, [128, 2, 512]) for i in range(2)]
        SQ = sb("SQ", 198, [128, 2, 512])
        rstd = sb("rstd", 202, [128, 512])
        rot = [sb(f"rot{i}", 156 + 2 * i, [128, 512]) for i in range(4)]
        spl = [sb(f"spl{i}", 164 + 2 * i, [128, 512], F32R) for i in range(4)]
        VV = sb("VV", 174, [128, 16, 16, 32])
        KS = [[sb(f"KS{i}{h}", 84 + 8 * i + 4 * h, [128, 1024], F32R) for h in range(2)] for i in range(3)]
        QS = [sb(f"QS{i}", 60 + 4 * i, [128, 1024], F32R) for i in range(4)]
        P = [sb(f"P{i}", 108 + 8 * i, [128, 2048]) for i in range(4)]
        OE = [sb(f"OE{i}", 140 + 2 * i, [128, 512]) for i in range(2)]
        NUM = [sb(f"NUM{i}", 28 + 8 * i, [128, 2, 1024]) for i in range(2)]
        DEN = [sb(f"DEN{i}", 44 + 8 * i, [128, 2, 1024]) for i in range(2)]
        OH = sb("OH", 144, [128, 2, 512], F32R)
        OL = sb("OL", 148, [128, 2, 512], F32R)
        PS = ctx.enter_context(nc.psum_tensor("PS", [128, 8, 512], F32))
        bank = [PS[:, i, :] for i in range(8)]
        scr = [nc.dram_tensor(n, (256, NT), F32R).ap() for n in ("scr_qh", "scr_ql", "scr_kh", "scr_kl")]

        def col(name, i=0):
            a = COLS[name][0] + i
            return cols[:, a:a + 1]

        def r32(ap):
            return ap.bitcast(F32)

        d_c = dsem("d_c")
        d_x = [dsem(f"d_x{c}") for c in range(NCH)]
        d_st = [dsem(f"d_st{i}") for i in range(2)]
        for c in range(NCH):
            t_x = d_x[c].start(S, X[:, :, c * 512:(c + 1) * 512], xT[:, :, c * 512:(c + 1) * 512])
        for t, d in ((cols, cols_d), (MASK, mask_d), (HAD, had_d), (IDN, ident_d), (COS, cos_d), (SIN, sin_d)):
            t_const = d_c.start(A, t[:, :], d)
        t_const = d_c.start(A, BKV[:, :], bkv_d)

        t_mean = V.do(lambda e: e.memset(MEAN[:, :], 1.0 / 256))
        t_ones = V.do(lambda e: e.memset(ONES[:, :], 1.0))
        for i in range(2):
            t_ve1 = V.do(lambda e, i=i: e.memset(ve[i][:, :, 128:129], 1.0))

        ps = Ring(bank[0:6])

        st_free = [None, None]
        st_n = [0]

        def stage(src, n):
            i = st_n[0] % 2
            st_n[0] += 1
            t = d_st[i].start(S, stg[i][:, 0:n], src, st_free[i])
            return i, t


        def mm(out, pairs, tokens, free=None, start=True, stop=True):
            T.wait(free, *tokens)
            for j, (l, r) in enumerate(pairs):
                f = lambda e, l=l, r=r, j=j: e.matmul(out, l, r, start=start and j == 0, stop=stop and j == len(pairs) - 1)
                if j == len(pairs) - 1:
                    return T.do(f)
                T.put(f)

        def three(wh, wl, xh, xl):
            return [(wh, xh), (wh, xl), (wl, xh)]

        def layernorm(c, t_in, t_free):
            sl = slice(c * 512, (c + 1) * 512)
            xc = XC[c % 2]
            m, free, i = ps.next()
            t_m = mm(m, [(MEAN[:, :], X[:, k, sl]) for k in range(2)], [t_mean, *t_in], free)
            for k in range(2):
                t_xc = V.do(lambda e, k=k: e.tensor_tensor(xc[:, k, :], X[:, k, sl], m, ALU.subtract), t_m, ln_free[c % 2])
            ps.free[i] = t_xc
            t_sq = A.do(lambda e: e.activation(SQ[:, :, :], xc[:, :, :], ACT.Square), t_xc, sq_free[0])
            v, free, i = ps.next()
            t_v = mm(v, [(MEAN[:, :], SQ[:, k, :]) for k in range(2)], [t_sq], free)
            sq_free[0] = t_v
            t_sd = A.do(lambda e: e.activation(rstd[:, :], v, ACT.Sqrt, bias=col("eps5")), t_v, t_const, rstd_free[0])
            ps.free[i] = t_sd
            t_r = V.do(lambda e: e.reciprocal(rstd[:, :], rstd[:, :]), t_sd)
            for k in range(2):
                t_n = V.do(lambda e, k=k: e.tensor_tensor(xc[:, k, :], xc[:, k, :], rstd[:, :], ALU.mult), t_r)
            rstd_free[0] = t_n
            t_h = A.do(lambda e: e.activation(XH[:, :, sl], xc[:, :, :], ACT.Copy), t_n, *t_free)
            t_l = G.do(lambda e: e.tensor_tensor(XL[:, :, sl], xc[:, :, :], r32(XH[:, :, sl]), ALU.subtract), t_h)
            ln_free[c % 2] = t_l
            return [t_h, t_l]

        ln_free = [None, None]
        sq_free = [None]
        rstd_free = [None]

        wi, t_w = stage(wa0, 2048)
        raw = stg[wi][:, :].rearrange("p (k n) -> p k n", k=2)
        t_wh = A.do(lambda e: e.activation(W0H[:, :, :], raw, ACT.Copy), t_w)
        t_wl = G.do(lambda e: e.tensor_tensor(W0L[:, :, :], raw, r32(W0H[:, :, :]), ALU.subtract), t_wh)
        st_free[wi] = t_wl
        t_w0 = [t_wh, t_wl]

        t_xn = []
        for c in range(NCH):
            t_xn.append(layernorm(c, [(d_x[c].sem, d_x[c].n)], []))

        tern_t = []
        for n, dst in enumerate((TU, TG, TD)):
            i, t_w = stage(tern[n], 2048)
            flat = dst[:, :, :].rearrange("p k n -> p (k n)")
            t_a = A.do(lambda e, i=i, flat=flat, n=n: e.activation(flat, stg[i][:, :], ACT.Abs, accum_out=s16[:, n:n + 1]), t_w)
            p, free, pi = ps.next()
            t_s = mm(p[:, 0:1], [(ONES[:, :], s16[:, n:n + 1])], [t_a, t_ones], free)
            t_sc = V.do(lambda e, n=n, p=p: e.tensor_scalar(s16[:, 3 + n:4 + n], p[:, 0:1], 1.0 / 262144, 1e-8, ALU.mult, ALU.add), t_s)
            ps.free[pi] = t_sc
            sc = s16[:, 3 + n:4 + n]
            hi, lo = s16[:, 10:11], s16[:, 11:12]
            t_hi = V.do(lambda e, sc=sc, hi=hi: e.tensor_scalar(hi, sc, 0.5, None, ALU.mult), t_sc)
            t_lo = V.do(lambda e, sc=sc, lo=lo: e.tensor_scalar(lo, sc, -0.5, None, ALU.mult))
            t_p = V.do(lambda e, i=i, flat=flat, lo=lo: e.tensor_scalar(flat, stg[i][:, :], lo, None, ALU.is_lt), t_lo, t_w)
            t_t = V.do(lambda e, i=i, flat=flat, hi=hi: e.scalar_tensor_tensor(flat, stg[i][:, :], hi, r32(flat), ALU.is_gt, ALU.subtract), t_p)
            st_free[i] = t_t
            tern_t.append(t_t)
        su, sgt, sdn, sgd = (s16[:, i:i + 1] for i in (3, 4, 5, 6))
        t_sgd = V.do(lambda e: e.tensor_tensor(sgd, sgt, sdn, ALU.mult), tern_t[2])

        zs_free = [None, None]
        q_t = []
        for c in range(NCH):
            sl = slice(c * 512, (c + 1) * 512)
            for m in range(2):
                p, free, pi = ps.next()
                pr = [x for k in range(2) for x in three(W0H[:, k, m * 128:(m + 1) * 128], W0L[:, k, m * 128:(m + 1) * 128],
                                                         XH[:, k, sl], XL[:, k, sl])]
                t_p = mm(p, pr, [*t_xn[c], *t_w0], free)
                j = m
                t_n = V.do(lambda e, p=p, m=m, j=j: e.tensor_scalar(zs[j][:, :], p, col("qb0", m), 0.0, ALU.add, ALU.min), t_p, t_const, zs_free[j])
                t_r = V.do(lambda e, p=p, m=m, sl=sl: e.tensor_scalar(QP[:, m, sl], p, col("qb0", m), 0.0, ALU.add, ALU.max))
                ps.free[pi] = t_r
                t_e = A.do(lambda e, j=j: e.activation(zs[j][:, :], zs[j][:, :], ACT.Exp), t_n)
                t_q = G.do(lambda e, j=j, m=m, sl=sl: e.tensor_tensor(QP[:, m, sl], zs[j][:, :], QP[:, m, sl], ALU.add), t_r, t_e)
                zs_free[j] = t_q
            q_t.append(t_q)

        kv_free = None
        kv_n = 0
        kv_mm = [None, None]
        at_free = [None, None]
        x_t = []
        for b in range(2):
            for i in range(8):
                tt = 8 * b + i
                j = tt % 2
                tk = slice(tt * 128, (tt + 1) * 128)
                p, free, pi = ps.next()
                pr = [x for k in range(2) for x in ((XH[:, k, tk], W0H[:, k, 256:768]), (XH[:, k, tk], W0L[:, k, 256:768]),
                                                    (XL[:, k, tk], W0H[:, k, 256:768]))]
                t_p = mm(p, pr, [*t_xn[tt // 4], *t_w0], free)
                t_z = V.do(lambda e, p=p, j=j: e.tensor_tensor(zk[j][:, :], p[:, 0:256], BKV[:, 0:256], ALU.add), t_p, t_const, kv_mm[j])
                t_v = V.do(lambda e, p=p, j=j: e.tensor_tensor(ve[j][:, :, 0:128], p[:, 256:512].rearrange("p (g n) -> p g n", g=2),
                                                              BKV[:, 256:512].rearrange("p (g n) -> p g n", g=2), ALU.add), t_p, kv_mm[j])
                ps.free[pi] = t_v
                t_e = G.do(lambda e, j=j: e.tensor_scalar(ek[j][:, :], zk[j][:, :], 0.0, None, ALU.min), t_z)
                t_e = A.do(lambda e, j=j: e.activation(ek[j][:, :], ek[j][:, :], ACT.Exp), t_e)
                t_r = G.do(lambda e, j=j: e.tensor_scalar(rk[j][:, :], zk[j][:, :], 0.0, None, ALU.max), t_z)
                t_k = V.do(lambda e, j=j: e.tensor_tensor(kp[j][:, :], ek[j][:, :], rk[j][:, :], ALU.add), t_e, t_r)
                for g in range(2):
                    kv_mm[j] = mm(bank[6 + g][:, 0:129], [(kp[j][:, g * 128:(g + 1) * 128], ve[j][:, g, :])], [t_k, t_v, t_ve1],
                                  kv_free if i == 0 else None, start=(i == 0), stop=(i == 7))
            t_b = V.do(lambda e: e.tensor_tensor(kvb[0][:, :], bank[6][:, 0:128], MASK[:, :], ALU.mult), kv_mm[1], *at_free)
            t_b = V.do(lambda e: e.tensor_scalar(zb[0][:, :], MASK[:, :], bank[6][:, 128:129], None, ALU.mult))
            t_b = V.do(lambda e: e.tensor_tensor(kvb[1][:, :], bank[7][:, 0:128], MASK[:, :], ALU.mult))
            t_b = V.do(lambda e: e.tensor_scalar(zb[1][:, :], MASK[:, :], bank[7][:, 128:129], None, ALU.mult))
            kv_free = t_b
            for cc in range(2):
                c = 2 * b + cc
                sl = slice(c * 512, (c + 1) * 512)
                for g in range(2):
                    pz, free, zi = ps.next()
                    t_z = mm(pz, [(zb[g][:, :], QP[:, g, sl])], [t_b, q_t[c]], free)
                    pn, free, ni = ps.next()
                    t_n = mm(pn, [(kvb[g][:, :], QP[:, g, sl])], [t_b, q_t[c]], free)
                    at_free[g] = t_n
                    t_zc = A.do(lambda e, pz=pz, g=g: e.activation(zs[g][:, :], pz, ACT.Identity, bias=col("eps")), t_z, zs_free[g])
                    ps.free[zi] = t_zc
                    t_rz = V.do(lambda e, g=g: e.reciprocal(zs[g][:, :], zs[g][:, :]), t_zc)
                    t_a = V.do(lambda e, g=g, pn=pn: e.tensor_tensor(at[:, g, :], pn, zs[g][:, :], ALU.mult),
                               t_rz, t_n, ah_free if (b or cc) else None)
                    ps.free[ni] = t_a
                    zs_free[g] = t_a
                t_h = A.do(lambda e: e.activation(AH[:, :, :], at[:, :, :], ACT.Copy), t_a, oj_free if (b or cc) else None)
                t_l = G.do(lambda e: e.tensor_tensor(AL[:, :, :], at[:, :, :], r32(AH[:, :, :]), ALU.subtract), t_h)
                ah_free = t_l
                for m in range(2):
                    p, free, pi = ps.next()
                    ms = slice(768 + m * 128, 768 + (m + 1) * 128)
                    pr = [x for k in range(2) for x in three(W0H[:, k, ms], W0L[:, k, ms], AH[:, k, :], AL[:, k, :])]
                    t_p = mm(p, pr, [t_h, t_l], free)
                    oj_free = t_p
                    t_x1 = V.do(lambda e, p=p, m=m, sl=sl: e.scalar_tensor_tensor(X[:, m, sl], p, col("ob0", m), X[:, m, sl], ALU.add, ALU.add), t_p)
                    ps.free[pi] = t_x1
                x_t.append(t_x1)
        t_att0 = t_x1
        t_att0_pe = oj_free

        f_hs = Ring(hh)
        f_sg = Ring(sg)
        bank_free = [kv_free, kv_free]

        def ffn(c, gate_mm, up_mm, tokens, gscale, uscale, down, down_tokens, out):
            nonlocal_t = []

            def down_mm(m, sl, th, tl):
                for d in range(2):
                    t = mm(bank[6 + d], down(m, d, hh[sl][:, :], hl[sl][:, :]), [th, tl, *down_tokens],
                           bank_free[d] if m == 0 else None, start=(m == 0), stop=(m == 7))
                f_hs.free[sl] = t
                return t

            for m in range(8):
                pg, free, gi = ps.next()
                t_g = mm(pg, gate_mm(m, c), tokens, free)
                pu, free, ui = ps.next()
                t_u = mm(pu, up_mm(m, c), tokens, free)
                s, s_free, si = f_sg.next()
                _, h_free, hi = f_hs.next()
                t_s = A.do(lambda e, s=s, pg=pg, m=m: e.activation(s[:, :], pg, ACT.Silu, scale=gscale(m)), t_g, s_free)
                ps.free[gi] = t_s
                t_h = V.do(lambda e, s=s, pu=pu, m=m: e.scalar_tensor_tensor(s[:, :], pu, uscale(m), s[:, :], ALU.mult, ALU.mult), t_u, t_s)
                ps.free[ui] = t_h
                t_hh = A.do(lambda e, s=s, hi=hi: e.activation(hh[hi][:, :], s[:, :], ACT.Copy), t_h, h_free)
                t_hl = G.do(lambda e, s=s, hi=hi: e.tensor_tensor(hl[hi][:, :], s[:, :], r32(hh[hi][:, :]), ALU.subtract), t_hh)
                f_sg.free[si] = t_hl
                nonlocal_t.append((m, hi, t_hh, t_hl))
                if m >= 2:
                    down_mm(*nonlocal_t[m - 2])
            down_mm(*nonlocal_t[6])
            t = down_mm(*nonlocal_t[7])
            for d in range(2):
                bank_free[d] = out(d, c, t)
            return bank_free[1]

        def wide(w_h, w_l, m0, c, two):
            sl = slice(c * 512, (c + 1) * 512)
            ms = slice(m0, m0 + 128)
            if two:
                return [x for k in range(2) for x in ((w_h[:, k, ms], XH[:, k, sl]), (w_h[:, k, ms], XL[:, k, sl]))]
            return [x for k in range(2) for x in three(w_h[:, k, ms], w_l[:, k, ms], XH[:, k, sl], XL[:, k, sl])]

        def out0(d, c, t):
            sl = slice(c * 512, (c + 1) * 512)
            return V.do(lambda e: e.scalar_tensor_tensor(X[:, d, sl], bank[6 + d], sgd, X[:, d, sl], ALU.mult, ALU.add), t, t_sgd, x_t[c])

        def prep_attn1():
            ts = []
            for src, n, H, L, ns in ((wa1[0], 640, W1H, W1L, slice(0, 640)), (wa1[1], 640, W1H, W1L, slice(640, 1280)), (wo1, 256, WOH, WOL, slice(0, 256))):
                i, t_w = stage(src, 2 * n)
                raw = stg[i][:, 0:2 * n].rearrange("p (k n) -> p k n", k=2)
                t_h = A.do(lambda e, raw=raw, ns=ns, H=H: e.activation(H[:, :, ns], raw, ACT.Copy), t_w, t_att0_pe)
                t_l = G.do(lambda e, raw=raw, ns=ns, H=H, L=L: e.tensor_tensor(L[:, :, ns], raw, r32(H[:, :, ns]), ALU.subtract), t_h)
                st_free[i] = t_l
                ts += [t_h, t_l]
            return ts

        def prep_ug(n):
            i, t_w = stage(wf1[n], 2048)
            raw = stg[i][:, :].rearrange("p (k n) -> p k n", k=2)
            ts = []
            for k in range(2):
                for h in range(2):
                    p, free, pi = ps.next()
                    hs = slice(h * 512, (h + 1) * 512)
                    ds = slice(n * 1024 + h * 512, n * 1024 + (h + 1) * 512)
                    t_p = mm(p, [(HAD[:, :], raw[:, 0, hs]), ((HADN if k else HAD)[:, :], raw[:, 1, hs])], [t_w, t_hadn], free)
                    t_h = A.do(lambda e, p=p, k=k, ds=ds: e.activation(UGH[:, k, ds], p, ACT.Copy, scale=s16[:, 8 + k:9 + k]), t_p, t_sus, t_att0, t_att0_pe)
                    t_l = V.do(lambda e, p=p, k=k, ds=ds: e.scalar_tensor_tensor(UGL[:, k, ds], p, s16[:, 8 + k:9 + k], r32(UGH[:, k, ds]), ALU.mult, ALU.subtract), t_h)
                    ps.free[pi] = t_l
                    ts += [t_h, t_l]
            st_free[i] = t_p
            return [ts[-1], ts[-2]]

        def prep_down():
            i, t_w = stage(wf1[2], 2048)
            a, bf = stg[i], stg[1 - i]
            t = t_w
            other = st_free[1 - i]
            for s in (1, 2, 4):
                av, bv = (z[:, :].rearrange("p (o t i) -> p o t i", t=2, i=256 * s) for z in (a, bf))
                t = G.do(lambda e, av=av, bv=bv: e.tensor_tensor(bv[:, :, 0, :], av[:, :, 0, :], av[:, :, 1, :], ALU.add), t, other)
                t = G.do(lambda e, av=av, bv=bv: e.tensor_tensor(bv[:, :, 1, :], av[:, :, 0, :], av[:, :, 1, :], ALU.subtract))
                a, bf = bf, a
            for q in range(4):
                p, free, pi = ps.next()
                t_p = mm(p, [(HAD[:, :], a[:, q * 512:(q + 1) * 512])], [t, t_const], free)
                parts = [(2 * q + r, p[:, r * 256:(r + 1) * 256], s16b[:, 2 * q + r:2 * q + r + 1]) for r in range(2)]
                for cc, pr, sc in parts:
                    t_h = A.do(lambda e, cc=cc, pr=pr, sc=sc: e.activation(DH[:, cc, :], pr, ACT.Copy, scale=sc), t_p, t_sus, t_att0, t_att0_pe)
                for cc, pr, sc in parts:
                    t_l = V.do(lambda e, cc=cc, pr=pr, sc=sc: e.scalar_tensor_tensor(DL[:, cc, :], pr, sc, r32(DH[:, cc, :]), ALU.mult, ALU.subtract), t_h)
                ps.free[pi] = t_l
            st_free[0] = st_free[1] = t_p
            return [t_h, t_l]

        s16b = sb("s16b", 27.75, [128, 8])
        t_sus = V.do(lambda e: e.tensor_scalar(s16[:, 8:10], cols[:, COLS["suu"][0]:COLS["suu"][0] + 2], 1.0 / 16, None, ALU.mult), t_const)
        t_sus = V.do(lambda e: e.tensor_scalar(s16b[:, :], cols[:, COLS["sud"][0]:COLS["sud"][0] + 8], 1.0 / 32, None, ALU.mult))
        t_hadn = V.do(lambda e: e.tensor_scalar(HADN[:, :], HAD[:, :], -1.0, None, ALU.mult))

        x1_t = []
        w1_t = f1_t = None
        for c in range(NCH):
            t = ffn(c, lambda m, c: wide(TU, None, m * 128, c, True),
                    lambda m, c: wide(TG, None, m * 128, c, True), [*t_xn[c], *tern_t],
                    lambda m: su, lambda m: 1.0,
                    lambda m, d, h, l: [(TD[:, m, d * 128:(d + 1) * 128], h), (TD[:, m, d * 128:(d + 1) * 128], l)],
                    [tern_t[2]], out0)
            x1_t.append(t)
            if c == 0:
                w1_t = prep_attn1()
            elif c == 1:
                f1_t = prep_ug(0)
            elif c == 2:
                f1_t += prep_ug(1)
                f1_t += prep_down()
        t_ffn0_pe = T.last()
        t_stage_done = st_free[0]

        t_xn = [layernorm(c, [x1_t[c]], [t_ffn0_pe]) for c in range(NCH)]

        d_scr = dsem("d_scr")
        rot_free = [None] * 4
        spl_free = [None] * 4
        nq = 0
        t_hid = t_ffn0_pe
        d_sp = [dsem(f"d_sp{i}") for i in range(4)]
        for c in range(NCH):
            sl = slice(c * 512, (c + 1) * 512)
            cs = slice((c % 2) * 512, (c % 2 + 1) * 512)
            for n in range(2):
                for m in range(2):
                    ri, si = 2 * (nq % 2), 2 * (nq % 2)
                    nq += 1
                    pp = []
                    for s in range(2):
                        p, free, pi = ps.next()
                        m0 = n * 512 + s * 256 + m * 128
                        t_p = mm(p, wide(W1H, W1L, m0, c, False), [*t_xn[c], *w1_t], free)
                        pp.append((p, pi, t_p))
                    a, bq = rot[ri], rot[ri + 1]
                    sc = 0.25 if n == 0 else 1.0
                    t_a = V.do(lambda e, p=pp[0][0], n=n, m=m, a=a, cs=cs: e.scalar_tensor_tensor(
                        a[:, :], p, col("qb1" if n == 0 else "kb1", m), COS[:, cs], ALU.add, ALU.mult), pp[0][2], rot_free[ri], t_hid, f_sg.free[0], f_sg.free[1], f_sg.free[2])
                    ps.free[pp[0][1]] = t_a
                    t_b = V.do(lambda e, p=pp[1][0], n=n, m=m, bq=bq, cs=cs: e.scalar_tensor_tensor(
                        bq[:, :], p, col("qsb1" if n == 0 else "ksb1", m), SIN[:, cs], ALU.add, ALU.mult), pp[1][2])
                    ps.free[pp[1][1]] = t_b
                    t_r = G.do(lambda e, a=a, bq=bq: e.tensor_tensor(a[:, :], a[:, :], bq[:, :], ALU.add), t_b)
                    sh, sl_ = spl[si], spl[si + 1]
                    t_h = A.do(lambda e, a=a, sh=sh, sc=sc: e.activation(sh[:, :], a[:, :], ACT.Copy, scale=sc), t_r, spl_free[si])
                    t_l = V.do(lambda e, a=a, sh=sh, sl_=sl_, sc=sc: e.scalar_tensor_tensor(sl_[:, :], a[:, :], sc, r32(sh[:, :]), ALU.mult, ALU.subtract), t_h, spl_free[si + 1])
                    rot_free[ri] = t_l
                    ms = slice(m * 128, (m + 1) * 128)
                    spl_free[si] = d_sp[si].start(S, scr[2 * n][ms, sl], sh[:, :], t_h)
                    spl_free[si + 1] = d_sp[si + 1].start(S, scr[2 * n + 1][ms, sl], sl_[:, :], t_l)
        t_scr = list(spl_free)

        t_v1 = V.do(lambda e: e.memset(VV[:, :, :, 16:32], 1.0), t_stage_done, ln_free[0], ln_free[1], sq_free[0], t_xn[3][0], t_xn[3][1])
        for tt in range(16):
            tk = slice(tt * 128, (tt + 1) * 128)
            p, free, pi = ps.next()
            pr = [x for k in range(2) for x in ((XH[:, k, tk], W1H[:, k, 1024:1280]), (XH[:, k, tk], W1L[:, k, 1024:1280]),
                                                (XL[:, k, tk], W1H[:, k, 1024:1280]))]
            t_p = mm(p[:, 0:256], pr, [*t_xn[tt // 4]], free)
            t_vv = A.do(lambda e, p=p, tt=tt: e.activation(VV[:, tt, :, 0:16], p[:, 0:256].rearrange("p (h d) -> p h d", h=16), ACT.Copy), t_p, t_v1)
            ps.free[pi] = t_vv
        t_v_pe = T.last()

        def out1(d, c, t):
            sl = slice(c * 512, (c + 1) * 512)
            return V.do(lambda e: e.scalar_tensor_tensor(X[:, d, sl], bank[6 + d], col("wsd", d), X[:, d, sl], ALU.mult, ALU.add), t)

        d_ks = [dsem(f"d_ks{i}") for i in range(3)]
        d_qs = [dsem(f"d_qs{i}") for i in range(4)]
        d_m = [dsem(f"d_m{i}") for i in range(2)]
        d_oe = [dsem(f"d_oe{i}") for i in range(2)]
        t_ki = [None] * 3
        for i in range(3):
            for h, row in enumerate(("rowa", "rowb")):
                t_ki[i] = V.do(lambda e, i=i, h=h, row=row: e.tensor_scalar(KS[i][h][:, :], COS[:, :], 0.0, col(row), ALU.mult, ALU.add), t_ffn0_pe)
        t_qi = [V.do(lambda e, i=i: e.memset(r32(QS[i][:, :]), 0.0), t_v_pe) for i in range(4)]
        qh, ql, kh, kl = scr
        k_tok = [None] * 16
        q_tok = [None] * 16

        def load(p, t_k, t_q):
            b, j = divmod(p, 8)
            ts = slice(b * 1024, (b + 1) * 1024)
            kslot, qslot = p % 3, p % 4
            S.wait(*t_scr, t_k, t_q)
            if p >= 4:
                S.wait(q_tok[p - 4])
                q_tok[p] = d_qs[qslot].start(S, QS[qslot][48:49, :], QS[qslot][49:50, :])
                q_tok[p] = d_qs[qslot].start(S, QS[qslot][112:113, :], QS[qslot][113:114, :])
            for h in range(2):
                fs = slice(32 * j + 16 * h, 32 * j + 16 * h + 16)
                for r, (qsrc, ksrc) in enumerate(((qh, kh), (qh, kl), (ql, kh))):
                    rows = slice(64 * h + 16 * r, 64 * h + 16 * r + 16)
                    k_tok[p] = d_ks[kslot].start(S, KS[kslot][h][rows, :], ksrc[fs, ts])
                    q_tok[p] = d_qs[qslot].start(S, QS[qslot][rows, :], qsrc[fs, ts])

        for p in range(3):
            load(p, t_ki[p], t_qi[p])

        for q in (A, V, G):
            q.wait(*t_scr)
        for c in range(NCH):
            ffn(c, lambda m, c: wide(UGH, UGL, 1024 + m * 128, c, False),
                lambda m, c: wide(UGH, UGL, m * 128, c, False), [*t_xn[c], *f1_t],
                lambda m: col("wsg", m), lambda m: col("wsu", m),
                lambda m, d, h, l: [(DH[:, m, d * 128:(d + 1) * 128], h), (DH[:, m, d * 128:(d + 1) * 128], l), (DL[:, m, d * 128:(d + 1) * 128], h)],
                f1_t, out1)
        t_ffn1_pe = T.last()
        t_ffn1_v = V.last()

        MX = Ring([0, 2])
        ST = Ring([4, 5, 6])
        MX.free = [t_ffn1_v] * 2
        ST.free = [t_ffn1_v] * 3
        T.wait(A.last(), G.last())
        pv_free = t_ffn1_v
        NP, LEAD, LAG = 16, 11, 2
        mx_free = [None] * 2
        mrow_free = [None] * 2
        max_tok = [None] * NP
        m_tok = [None] * NP
        st_last = [None] * NP
        p_tok = {}
        p_free = [t_ffn1_pe] * 4
        oe_free = [None, None]
        num_tok = [None, None]

        def max_tile(p, u):
            h, qt = divmod(u, 8)
            i, free, mi = MX.next()
            T.wait(free, k_tok[p], q_tok[p], t_ki[p % 3], t_qi[p % 4])
            for half in range(2):
                f = lambda e, half=half: e.matmul(PS[:, i + half, :], QS[p % 4][:, qt * 128:(qt + 1) * 128],
                                                  KS[p % 3][h][:, half * 512:(half + 1) * 512], start=True, stop=True)
                if half == 0:
                    T.put(f)
                else:
                    t = T.do(f)
            MX.free[mi] = V.do(lambda e: e.tensor_reduce(mx[p % 2][:, u:u + 1], PS[:, i:i + 2, :], AX.XY, ALU.max), t,
                               mx_free[p % 2] if u == 0 else None)
            max_tok[p] = MX.free[mi]
            return t

        def max_rows(p, t_pe):
            i, free, si = ST.next()
            t = T.do(lambda e: e.transpose(PS[0:16, i, 0:128], mx[p % 2][:, :], IDN[:, :]), free, max_tok[p])
            mx_free[p % 2] = t
            t = A.do(lambda e: e.activation(mrow[p % 2][:, :], PS[0:16, i, 0:128], ACT.Copy, scale=-1.0), t, mrow_free[p % 2])
            ST.free[si] = t
            for h in range(2):
                r = 48 + 64 * h
                m_tok[p] = d_m[p % 2].start(S, QS[p % 4][r:r + 1, :].rearrange("a (q n) -> a q n", q=8), mrow[p % 2][8 * h:8 * h + 8, :], t, t_pe)
            mrow_free[p % 2] = m_tok[p]

        def scores(s, c):
            p, kt = divmod(s, 8)
            h, half = divmod(c, 2)
            i, free, si = ST.next()
            t = T.do(lambda e: e.matmul(PS[:, i, :], KS[p % 3][h][:, kt * 128:(kt + 1) * 128], QS[p % 4][:, half * 512:(half + 1) * 512],
                                        start=True, stop=True), free, m_tok[p])
            st_last[p] = t
            ST.free[si] = A.do(lambda e: e.activation(P[s % 4][:, c * 512:(c + 1) * 512], PS[:, i, :], ACT.Exp), t, p_free[s % 4] if c == 0 else None)
            p_tok[s] = ST.free[si]

        def values(s):
            nonlocal pv_free
            p, kt = divmod(s, 8)
            b, j = divmod(p, 8)
            T.wait(p_tok[s], t_vv, pv_free if kt == 0 else None)
            for c in range(4):
                f = lambda e, c=c: e.matmul(PS[32 * c:32 * c + 32, 7, :], VV[:, 8 * b + kt, 2 * j + c // 2, :], P[s % 4][:, c * 512:(c + 1) * 512],
                                            start=(kt == 0), stop=(kt == 7), tile_position=(0, 32 * c))
                if c < 3:
                    T.put(f)
                else:
                    t = T.do(f)
            p_free[s % 4] = t
            if kt == 7:
                o = p % 2
                pv_free = A.do(lambda e: e.activation(OE[o][:, :], PS[:, 7, :], ACT.Copy), t, oe_free[o])
                for c in range(4):
                    h, half = divmod(c, 2)
                    row = 16 * ((2 * j + h) % 8)
                    f = (2 * j + h) // 8
                    for dst, off in ((NUM, 0), (DEN, 16)):
                        oe_free[o] = d_oe[o].start(S, dst[b][row:row + 16, f, half * 512:(half + 1) * 512],
                                                   OE[o][32 * c + off:32 * c + off + 16, :], pv_free, t_ffn1_pe)
                num_tok[b] = (num_tok[b] or []) + [oe_free[o]]

        t_pe = [None] * NP
        for s in range(-LEAD, 8 * NP + LAG):
            ms = s + LEAD
            live = 0 <= s < 8 * NP
            maxing = ms < 8 * NP
            if 1 <= ms // 8 <= NP and ms % 8 == 0:
                max_rows(ms // 8 - 1, t_pe[ms // 8 - 1])
            for q in range(2):
                if live:
                    scores(s, 2 * q)
                if maxing:
                    t_pe[ms // 8] = max_tile(ms // 8, 2 * (ms % 8) + q)
                if live:
                    scores(s, 2 * q + 1)
            if s - LAG >= 0:
                values(s - LAG)
            if s >= 0 and s % 8 == 7 and s // 8 + 3 < NP:
                load(s // 8 + 3, st_last[s // 8], st_last[s // 8 - 1] if s // 8 >= 1 else None)

        d_y = dsem("d_y")
        PR = Ring([0, 1, 2, 3])
        PR.free = [max_tok[NP - 1]] * 4
        t_pr = None
        for b in range(2):
            for cc in range(2):
                c = 2 * b + cc
                sl = slice(c * 512, (c + 1) * 512)
                hs = slice(cc * 512, (cc + 1) * 512)
                t_d = V.do(lambda e, b=b, hs=hs: e.reciprocal(DEN[b][:, :, hs], DEN[b][:, :, hs]), *num_tok[b])
                t_n = V.do(lambda e, b=b, hs=hs: e.tensor_tensor(NUM[b][:, :, hs], NUM[b][:, :, hs], DEN[b][:, :, hs], ALU.mult), t_d)
                ts = []
                for k in range(2):
                    t_h = A.do(lambda e, b=b, hs=hs, k=k: e.activation(OH[:, k, :], NUM[b][:, k, hs], ACT.Identity, bias=col("vb1", k)), t_n, t_pr)
                    t_l = V.do(lambda e, b=b, hs=hs, k=k: e.scalar_tensor_tensor(OL[:, k, :], NUM[b][:, k, hs], col("vb1", k), r32(OH[:, k, :]), ALU.add, ALU.subtract), t_h, t_pr)
                    ts += [t_h, t_l]
                for m in range(2):
                    i, free, pi = PR.next()
                    ms = slice(m * 128, (m + 1) * 128)
                    t_p = mm(PS[:, i, :], [x for k in range(2) for x in three(WOH[:, k, ms], WOL[:, k, ms], OH[:, k, :], OL[:, k, :])], ts, free)
                    t_o = V.do(lambda e, m=m, sl=sl, i=i: e.scalar_tensor_tensor(X[:, m, sl], PS[:, i, :], col("ob1", m), X[:, m, sl], ALU.add, ALU.add), t_p)
                    PR.free[pi] = t_o
                    t_y = d_y.start(S, yT[:, m, sl], X[:, m, sl], t_o)
                t_pr = t_p
        S.wait(t_y)

        block = ctx.enter_context(nc.Block())

        @block.sync
        def _(e):
            S.run(e)

        @block.scalar
        def _(e):
            A.run(e)

        @block.vector
        def _(e):
            V.run(e)

        @block.gpsimd
        def _(e):
            G.run(e)

        @block.tensor
        def _(e):
            T.run(e)


def hadamard(n):
    import numpy as np
    h = np.ones((1, 1), np.float32)
    while h.shape[0] < n:
        h = np.block([[h, h], [h, -h]])
    return np.ascontiguousarray(h, np.float32)


def kernel(**inp):
    import numpy as np
    import concourse.bacc as bacc
    from concourse.bass_utils import run_bass_kernel_spmd as run

    inp = {k: np.asarray(v) for k, v in inp.items()}

    def fold(w):
        n, d = w.shape
        return w.T.reshape(d // 128, 128, n).transpose(1, 0, 2)

    def flat(w):
        return np.ascontiguousarray(w.reshape(128, -1))

    swap = np.arange(256).reshape(16, 2, 8)[:, ::-1].reshape(-1)
    x = inp["L0_attn_hidden_states"]
    xT = np.ascontiguousarray(fold(x.reshape(NT, 256)))
    wa0 = flat(np.concatenate([fold(inp[f"L0_attn_{n}_w"]) for n in "qkvo"], axis=2))
    tern = [flat(fold(inp[f"L0_ffn_W_{n}"])) for n in ("up", "gate", "down")]
    q, k, v = (inp[f"L1_attn_{n}_w"] for n in "qkv")
    wa = fold(np.concatenate([q, q[swap], k, k[swap], v], axis=0))
    wa1 = [flat(wa[:, :, :640]), flat(wa[:, :, 640:])]
    wo1 = flat(fold(inp["L1_attn_out_w"]))
    wf1 = [flat(fold(inp[f"L1_ffn_W_{n}"])) for n in ("up", "gate", "down")]

    def cut(a):
        return a.reshape(-1, 128).T

    qb, kb = inp["L1_attn_q_b"], inp["L1_attn_k_b"]
    ws = inp["L1_ffn_Wscale_ug"]
    part = np.arange(128)
    cols = np.ascontiguousarray(np.concatenate([
        cut(inp["L0_attn_q_b"]), cut(inp["L0_attn_o_b"]), cut(qb), cut(qb[swap]), cut(kb), cut(kb[swap]),
        cut(inp["L1_attn_v_b"]), cut(inp["L1_attn_out_b"]), cut(inp["L1_ffn_SU_ug"]), cut(inp["L1_ffn_SU_dp"]),
        cut(ws[:1024]), cut(ws[1024:]), cut(inp["L1_ffn_Wscale_dp"]),
        (part == 48).astype(np.float32)[:, None], (part == 112).astype(np.float32)[:, None],
        np.full((128, 1), 1e-6, np.float32), np.full((128, 1), 1e-5, np.float32)], axis=1))
    bkv = np.ascontiguousarray(np.broadcast_to(np.concatenate([inp["L0_attn_k_b"], inp["L0_attn_v_b"]])[None, :], (128, 512)))
    inv = (1.0 / np.float32(10000.0) ** (np.arange(0, 16, 2, dtype=np.float32) / np.float32(16))).astype(np.float32)
    fr = np.arange(1024, dtype=np.float32)[:, None] * inv[None, :]
    emb = np.concatenate([fr, fr], axis=1).astype(np.float32)
    sign = np.where(np.arange(16) < 8, -1.0, 1.0).astype(np.float32)
    cos = np.ascontiguousarray(np.tile(np.cos(emb).T, (8, 1)).astype(np.float32))
    sin = np.ascontiguousarray(np.tile((np.sin(emb) * sign).T, (8, 1)).astype(np.float32))
    mask = (part[:, None] // 16 == part[None, :] // 16).astype(np.float32)
    arrays = dict(xT=xT, wa0=wa0, wa1a=wa1[0], wa1b=wa1[1], wo1=wo1, cols=cols, bkv=bkv, cos=cos, sin=sin, had=hadamard(128),
                  mask=mask, ident=np.eye(128, dtype=np.float32))
    for i in range(3):
        arrays[f"tern{i}"] = tern[i]
        arrays[f"wf1{i}"] = wf1[i]
    arrays = {f"in_{n}": a for n, a in arrays.items()}

    nc = bacc.Bacc("TRN2", target_bir_lowering=False, num_devices=1)
    t = {n: nc.dram_tensor(n, a.shape, F32, kind="ExternalInput").ap() for n, a in arrays.items()}
    y = nc.dram_tensor("out_y", (128, 2, NT), F32, kind="ExternalOutput").ap()
    program(nc, t["in_xT"], t["in_wa0"], [t[f"in_tern{i}"] for i in range(3)], [t["in_wa1a"], t["in_wa1b"]], t["in_wo1"],
            [t[f"in_wf1{i}"] for i in range(3)], t["in_cols"], t["in_bkv"], t["in_cos"], t["in_sin"], t["in_had"], t["in_mask"],
            t["in_ident"], y)
    r = run(nc, [arrays], core_ids=[0])
    out = np.asarray(r.results[0]["out_y"])
    return np.ascontiguousarray(out.transpose(2, 1, 0).reshape(2, 1024, 256))
```

```python
from contextlib import ExitStack

import concourse.bass as bass
from concourse import mybir

F32 = mybir.dt.float32
F32R = mybir.dt.float32r
ALU = mybir.AluOpType
ACT = mybir.ActivationFunctionType
AX = mybir.AxisListType

NT = 2048
NCH = 4
KB = 1024

RATE0 = 2.0
RATE1 = 1.5

COLS = dict(qb0=(0, 2), ob0=(2, 2), qb1=(4, 2), kb1=(8, 2), vb1=(12, 2), ob1=(14, 2),
            suu=(16, 2), sud=(18, 8), wsu=(26, 8), wsg=(34, 8), wsd=(42, 2), rowa=(44, 1), rowb=(45, 1), eps=(46, 1), eps5=(47, 1))
NCOL = 48


class Queue:

    def __init__(self, sem):
        self.sem, self.n, self.ops, self.seen = sem, 0, [], {}

    def wait(self, *tokens):
        for t in tokens:
            if t is None:
                continue
            sem, v = t
            if self.seen.get(sem.name, 0) < v:
                self.seen[sem.name] = v
                self.ops.append(lambda e, sem=sem, v=v: e.wait_ge(sem, v))

    def do(self, f, *tokens):
        self.wait(*tokens)
        self.n += 1
        self.ops.append(lambda e: f(e).then_inc(self.sem, 1))
        return self.sem, self.n

    def put(self, f, *tokens):
        self.wait(*tokens)
        self.ops.append(f)

    def last(self):
        return (self.sem, self.n) if self.n else None

    def run(self, e):
        for f in self.ops:
            f(e)


class Arrivals:

    def __init__(self, sem):
        self.sem, self.n = sem, 0

    def start(self, q, out, in_, *tokens):
        self.n += 16
        out, in_ = (a.bitcast(F32) if a.dtype == F32R else a for a in (out, in_))
        q.put(lambda e: e.dma_start(out, in_).then_inc(self.sem, 16), *tokens)
        return self.sem, self.n


class Ring:

    def __init__(self, slots):
        self.slots, self.free, self.i = slots, [None] * len(slots), -1

    def next(self):
        self.i = (self.i + 1) % len(self.slots)
        return self.slots[self.i], self.free[self.i], self.i


def program(nc, xT, wa0, tern, wa1, wo1, wf1, cols_d, bkv_d, cos_d, sin_d, had_d, mask_d, ident_d, pad_d, yT):
    with ExitStack() as ctx:
        def sem(name):
            return ctx.enter_context(nc.semaphore(name))

        base = -(-nc.sbuf_base // 32) * 32

        def sb(name, kb, shape, dt=F32):
            return nc.alloc_sbuf_tensor_at(name, shape, dt, offset=base + int(kb * KB))

        V, A, G, T, S = (Queue(sem(n)) for n in ("s_dve", "s_act", "s_pool", "s_pe", "s_sp"))

        def dsem(name):
            return Arrivals(sem(name))

        X = sb("X", 0, [128, 2, NT])
        COS = sb("COS", 16, [128, 1024])
        SIN = sb("SIN", 20, [128, 1024])
        cols = sb("cols", 24, [128, NCOL])
        s16 = sb("s16", 24.25, [128, 16])
        HAD = sb("HAD", 24.5, [128, 128])
        HADN = sb("HADN", 25, [128, 128])
        IDN = sb("IDN", 25.5, [128, 128])
        MASK = sb("MASK", 26, [128, 128])
        MEAN = sb("MEAN", 26.5, [128, 128])
        ONES = sb("ONES", 27, [128, 128])
        mx = [sb(f"mx{i}", 27.5 + i / 16, [128, 16]) for i in range(2)]
        mrow = [sb(f"mrow{i}", 206 + i / 2, [16, 128], F32R) for i in range(2)]
        XH = sb("XH", 28, [128, 2, NT], F32R)
        XL = sb("XL", 44, [128, 2, NT], F32R)
        W0H = sb("W0H", 60, [128, 2, 1024], F32R)
        W0L = sb("W0L", 68, [128, 2, 1024], F32R)
        W1H = sb("W1H", 60, [128, 2, 768], F32R)
        W1L = sb("W1L", 66, [128, 2, 768], F32R)
        WOH = sb("WOH", 80, [128, 2, 256], F32R)
        WOL = sb("WOL", 82, [128, 2, 256], F32R)
        TU = sb("TU", 84, [128, 2, 1024], F32R)
        TG = sb("TG", 92, [128, 2, 1024], F32R)
        TD = sb("TD", 100, [128, 8, 256], F32R)
        QP = sb("QP", 108, [128, 2, NT])
        zk = [sb(f"zk{i}", 124 + i, [128, 256]) for i in range(4)]
        ek = [sb(f"ek{i}", 128 + i, [128, 256]) for i in range(4)]
        ve = [sb(f"ve{i}", 132 + 1.25 * i, [128, 2, 129]) for i in range(4)]
        kvb = [sb(f"kvb{i}", 137 + i / 2, [128, 128]) for i in range(2)]
        zb = [sb(f"zb{i}", 138 + i / 2, [128, 8]) for i in range(2)]
        zs = [sb(f"zs{i}", 139 + 2 * i, [128, 512]) for i in range(2)]
        at = sb("at", 143, [128, 2, 512])
        AH = sb("AH", 147, [128, 2, 512], F32R)
        AL = sb("AL", 151, [128, 2, 512], F32R)
        BKV = sb("BKV", 204, [128, 512])
        UGH = sb("UGH", 108, [128, 2, 2048], F32R)
        UGL = sb("UGL", 124, [128, 2, 2048], F32R)
        DH = sb("DH", 140, [128, 8, 256], F32R)
        DL = sb("DL", 148, [128, 8, 256], F32R)
        hh = [sb(f"hh{i}", (156, 158, 160, 76)[i], [128, 512], F32R) for i in range(4)]
        hl = [sb(f"hl{i}", (162, 164, 166, 78)[i], [128, 512], F32R) for i in range(4)]
        sg = [sb(f"sg{i}", 168 + 2 * i, [128, 512]) for i in range(3)]
        stg = [sb(f"stg{i}", 174 + 8 * i, [128, 2048]) for i in range(2)]
        XC = [sb(f"XC{i}", (190, 194, 156, 160)[i], [128, 2, 512]) for i in range(4)]
        SQ = [sb(f"SQ{i}", (198, 164, 72)[i], [128, 2, 512]) for i in range(3)]
        rb = [sb(f"rb{i}", 198 + 2 * i, [128, 512]) for i in range(2)]
        stg2 = sb("stg2", 190, [128, 2048])[:, :]
        rstd = [sb(f"rstd{i}", 202 + i / 32, [128, 4]) for i in range(2)]
        rz = [sb(f"rz{i}", 202.5 + i / 8, [128, 32]) for i in range(2)]
        rot = [sb(f"rot{i}", 84 + 2 * i, [128, 512]) for i in range(4)]
        spl = [sb(f"spl{i}", 92 + 2 * i, [128, 512], F32R) for i in range(4)]
        VV = sb("VV", 174, [128, 16, 16, 32])
        KS = [[sb(f"KS{i}{h}", (100, 16, 84)[i] + 4 * h, [128, 1024], F32R) for h in range(2)] for i in range(3)]
        QS = [sb(f"QS{i}", (72, 60, 64, 68)[i], [128, 1024], F32R) for i in range(4)]
        P = [sb(f"P{i}", 108 + 8 * i, [128, 2048]) for i in range(4)]
        OE = [sb(f"OE{i}", 140 + 2 * i, [128, 512]) for i in range(2)]
        NUM = [sb(f"NUM{i}", 28 + 4 * i, [128, 1024]) for i in range(2)]
        DEN = [sb(f"DEN{i}", 36 + 4 * i, [128, 1024]) for i in range(2)]
        OH = [sb(f"OH{i}", 44 + 4 * i, [128, 1024], F32R) for i in range(2)]
        OL = [sb(f"OL{i}", 52 + 4 * i, [128, 1024], F32R) for i in range(2)]
        RC = [sb(f"RC{i}", 150 + i / 8, [128, 16]) for i in range(2)]
        PS = ctx.enter_context(nc.psum_tensor("PS", [128, 8, 512], F32))
        bank = [PS[:, i, :] for i in range(8)]
        scr_q, scr_k = (nc.dram_tensor(n, (16, 64, NT), F32).ap() for n in ("scr_q", "scr_k"))
        scr_o = nc.dram_tensor("scr_o", (16, 4, 32, 512), F32).ap()
        scr_r = nc.dram_tensor("scr_r", (16, 4, 512), F32).ap()

        def col(name, i=0):
            a = COLS[name][0] + i
            return cols[:, a:a + 1]

        def r32(ap):
            return ap.bitcast(F32)

        d_c = dsem("d_c")
        d_x = [dsem(f"d_x{c}") for c in range(NCH)]
        d_st = [dsem(f"d_st{i}") for i in range(2)]
        d_cols = dsem("d_cols")
        t_cols = d_cols.start(A, cols[:, :], cols_d)
        for c in range(NCH):
            t_x = d_x[c].start(S, X[:, :, c * 512:(c + 1) * 512], xT[:, :, c * 512:(c + 1) * 512])
        for t, d in ((IDN, ident_d), (MASK, mask_d), (HAD, had_d)):
            t_const = d_c.start(A, t[:, :], d)
        t_const = d_c.start(A, BKV[:, :], bkv_d)

        t_mean = V.do(lambda e: e.memset(MEAN[:, :], 1.0 / 256))
        t_ones = V.do(lambda e: e.memset(ONES[:, :], 1.0))
        for i in range(4):
            t_ve1 = V.do(lambda e, i=i: e.memset(ve[i][:, :, 128:129], 1.0))

        ps = Ring(bank[0:2])
        pf = Ring(bank[3:6])

        st_free = [None, None]
        st_n = [0]

        def stage(src, n):
            i = st_n[0] % 2
            st_n[0] += 1
            t = d_st[i].start(S, stg[i][:, 0:n], src, st_free[i])
            return i, t


        def mm(out, pairs, tokens, free=None, start=True, stop=True):
            T.wait(free, *tokens)
            for j, (l, r) in enumerate(pairs):
                f = lambda e, l=l, r=r, j=j: e.matmul(out, l, r, start=start and j == 0, stop=stop and j == len(pairs) - 1)
                if j == len(pairs) - 1:
                    return T.do(f)
                T.put(f)

        def three(wh, wl, xh, xl):
            return [(wh, xh), (wh, xl), (wl, xh)]

        t_xn = {}
        t_x = {}
        ln_free = [None] * 4
        sq_free = [None] * 3
        rstd_free = [None] * 2

        def layernorm(c, t_in, t_free, xi, qi, ri, ring):
            sl = slice(c * 512, (c + 1) * 512)
            xc, sq, rs = XC[xi], SQ[qi], rstd[ri]
            m, free, i = ps.next()
            t_m = mm(m, [(MEAN[:, :], X[:, k, sl]) for k in range(2)], [t_mean, *t_in], free)
            for k in range(2):
                t_xc = V.do(lambda e, k=k: e.tensor_tensor(xc[:, k, :], X[:, k, sl], m, ALU.subtract), t_m, ln_free[xi])
            ps.free[i] = t_xc
            t_sq = A.do(lambda e: e.activation(sq[:, :, :], xc[:, :, :], ACT.Square), t_xc, sq_free[qi])
            yield
            v, free, i = ring.next()
            for j in range(4):
                t_v = mm(v[:, j:j + 1], [(sq[:, k, j * 128:(j + 1) * 128], MEAN[:, 0:1]) for k in range(2)], [t_sq], free)
            sq_free[qi] = t_v
            t_sd = A.do(lambda e, v=v: e.activation(rs[:, :], v[:, 0:4], ACT.Sqrt, bias=col("eps5")), t_v, t_cols, rstd_free[ri])
            ring.free[i] = t_sd
            t_r = V.do(lambda e: e.reciprocal(rs[:, :], rs[:, :]), t_sd)
            yield
            w, free, i = ring.next()
            for j in range(4):
                t_b = mm(w[:, j * 128:(j + 1) * 128], [(rs[:, j:j + 1].broadcast_to([128, 128]), IDN[:, :])], [t_r, t_const], free)
            rstd_free[ri] = t_b
            for k in range(2):
                t_n = V.do(lambda e, k=k: e.tensor_tensor(xc[:, k, :], xc[:, k, :], w, ALU.mult), t_b)
            ring.free[i] = t_n
            t_h = A.do(lambda e: e.activation(XH[:, :, sl], xc[:, :, :], ACT.Copy), t_n, t_free())
            t_l = G.do(lambda e: e.tensor_tensor(XL[:, :, sl], xc[:, :, :], r32(XH[:, :, sl]), ALU.subtract), t_h)
            ln_free[xi] = t_l
            t_xn[c] = [t_h, t_l]
            yield

        def run(g):
            for _ in g:
                pass

        def weave(main, side, rate):
            due = 0.0
            for _ in main:
                due += rate
                while due >= 1:
                    due -= 1
                    next(side, None)

        tern_t = {}

        def ternary(n, dst):
            i, t_w = stage(tern[n], 2048)
            flat = dst[:, :, :].rearrange("p k n -> p (k n)")
            t_a = A.do(lambda e: e.activation(flat, stg[i][:, :], ACT.Abs, accum_out=s16[:, n:n + 1]), t_w)
            yield
            p, free, pi = ps.next()
            t_s = mm(p[:, 0:1], [(ONES[:, :], s16[:, n:n + 1])], [t_a, t_ones], free)
            sc, hi, lo = (s16[:, j + n:j + n + 1] for j in (3, 10, 13))
            t_sc = V.do(lambda e: e.tensor_scalar(sc, p[:, 0:1], 1.0 / 262144, 1e-8, ALU.mult, ALU.add), t_s)
            ps.free[pi] = t_sc
            t_hi = V.do(lambda e: e.tensor_scalar(hi, sc, 0.5, None, ALU.mult), t_sc)
            t_lo = V.do(lambda e: e.tensor_scalar(lo, sc, -0.5, None, ALU.mult))
            t_p = V.do(lambda e: e.tensor_scalar(flat, stg[i][:, :], lo, None, ALU.is_lt), t_lo, t_w)
            t_t = V.do(lambda e: e.scalar_tensor_tensor(flat, stg[i][:, :], hi, r32(flat), ALU.is_gt, ALU.subtract), t_p)
            st_free[i] = t_t
            tern_t[n] = t_t
            yield

        ln0 = [layernorm(c, [(d_x[c].sem, d_x[c].n)], lambda: None, c, c % 2, c % 2, pf) for c in range(NCH)]
        wi, t_w = stage(wa0, 2048)
        raw0 = stg[wi][:, :].rearrange("p (k n) -> p k n", k=2)
        for i in (0, 1, 0, 2):
            next(ln0[i])
        t_wh = A.do(lambda e: e.activation(W0H[:, :, :], raw0, ACT.Copy), t_w)
        t_wl = V.do(lambda e: e.tensor_tensor(W0L[:, :, :], raw0, r32(W0H[:, :, :]), ALU.subtract), t_wh)
        st_free[wi] = t_wl
        t_w0 = [t_wh, t_wl]
        tn = [ternary(n, t) for n, t in enumerate((TU, TG, TD))]
        for i in (1, 0, 3, 2, 1):
            next(ln0[i])
        next(tn[0])
        for i in (3, 2, 3):
            next(ln0[i])
        su, sgt, sdn, sgd, suh = (s16[:, i:i + 1] for i in (3, 4, 5, 6, 7))
        tok = {}

        zs_free = [None, None]
        rz_free, rb_free = [None, None], [None, None]
        q_t = {}
        kv_bank = bank[2]
        kvt = {"kv_free": None, "ve": [None] * 4, "at": [None, None], "at_v": None, "oj": None, "b": None}
        kin = {}

        def q_unit(c, m):
            sl = slice(c * 512, (c + 1) * 512)
            p, free, pi = ps.next()
            ms = slice(m * 128, (m + 1) * 128)
            t_p = mm(p, [x for k in range(2) for x in three(W0H[:, k, ms], W0L[:, k, ms], XH[:, k, sl], XL[:, k, sl])],
                     [*t_xn[c], *t_w0], free)
            t_n = V.do(lambda e: e.tensor_scalar(zs[m][:, :], p, col("qb0", m), 0.0, ALU.add, ALU.min), t_p, t_const, zs_free[m])
            t_r = V.do(lambda e: e.tensor_scalar(QP[:, m, sl], p, col("qb0", m), 0.0, ALU.add, ALU.max))
            ps.free[pi] = t_r
            t_e = A.do(lambda e: e.activation(zs[m][:, :], zs[m][:, :], ACT.Exp), t_n)
            q_t[c, m] = G.do(lambda e: e.tensor_tensor(QP[:, m, sl], zs[m][:, :], QP[:, m, sl], ALU.add), t_r, t_e)
            zs_free[m] = q_t[c, m]

        def kv_in(tt):
            j = tt % 4
            tk = slice(tt * 128, (tt + 1) * 128)
            p, free, pi = ps.next()
            t_p = mm(p, [x for k in range(2) for x in ((XH[:, k, tk], W0H[:, k, 256:768]), (XH[:, k, tk], W0L[:, k, 256:768]),
                                                       (XL[:, k, tk], W0H[:, k, 256:768]))], [*t_xn[tt // 4], *t_w0], free)
            t_z = V.do(lambda e: e.tensor_tensor(zk[j][:, :], p[:, 0:256], BKV[:, 0:256], ALU.add), t_p, t_const, kvt["ve"][j])
            t_v = V.do(lambda e: e.tensor_tensor(ve[j][:, :, 0:128], p[:, 256:512].rearrange("p (g n) -> p g n", g=2),
                                                 BKV[:, 256:512].rearrange("p (g n) -> p g n", g=2), ALU.add))
            ps.free[pi] = t_v
            t_m = G.do(lambda e: e.tensor_scalar(ek[j][:, :], zk[j][:, :], 0.0, None, ALU.min), t_z)
            t_e = A.do(lambda e: e.activation(ek[j][:, :], ek[j][:, :], ACT.Exp), t_m)
            t_r = G.do(lambda e: e.tensor_scalar(zk[j][:, :], zk[j][:, :], 0.0, None, ALU.max))
            t_k = G.do(lambda e: e.tensor_tensor(zk[j][:, :], ek[j][:, :], zk[j][:, :], ALU.add), t_e, t_r)
            kin[tt] = (t_k, t_v)

        def kv_out(tt):
            j, i = tt % 4, tt % 8
            T.wait(*kin[tt], t_ve1, kvt["kv_free"] if i == 0 else None)
            for g in range(2):
                f = lambda e, g=g: e.matmul(kv_bank[:, g * 129:(g + 1) * 129], zk[j][:, g * 128:(g + 1) * 128], ve[j][:, g, :],
                                            start=(i == 0 and g == 0), stop=(i == 7), skip_group_check=True)
                if g == 0:
                    T.put(f)
                else:
                    kvt["ve"][j] = T.do(f)

        def kv_sums():
            t = kvt["ve"][3]
            V.wait(t, *kvt["at"])
            for g in range(2):
                V.do(lambda e, g=g: e.tensor_tensor(kvb[g][:, :], kv_bank[:, g * 129:g * 129 + 128], MASK[:, :], ALU.mult))
                t = V.do(lambda e, g=g: e.tensor_scalar(zb[g][:, :], MASK[:, 0:128:16], kv_bank[:, g * 129 + 128:g * 129 + 129], None, ALU.mult))
            kvt["kv_free"] = kvt["b"] = t

        def att_a(c, g):
            sl = slice(c * 512, (c + 1) * 512)
            pz, z_free, zi = ps.next()
            for j in range(4):
                js = slice(c * 512 + j * 128, c * 512 + (j + 1) * 128)
                t_z = mm(pz[:, j * 8:(j + 1) * 8], [(QP[:, g, js], zb[g][:, :])], [kvt["b"], q_t[c, g]], z_free)
            t_rz = V.do(lambda e: e.tensor_scalar(rz[g][:, :], pz[:, 0:32], 1e-6, None, ALU.add), t_z, rz_free[g])
            t_rz = V.do(lambda e: e.reciprocal(rz[g][:, :], rz[g][:, :]), t_rz)
            t_rb = A.do(lambda e: e.activation(rb[g][:, :].rearrange("p (h o) -> p h o", o=16),
                                               rz[g][:, :].rearrange("p (h o) -> p h o", o=1).broadcast_to([128, 32, 16]), ACT.Copy), t_rz, rb_free[g])
            rz_free[g] = t_rb
            pn, free, ni = ps.next()
            t_n = mm(pn, [(kvb[g][:, :], QP[:, g, sl])], [], free)
            kvt["at"][g] = t_n
            t_nc = A.do(lambda e: e.activation(zs[g][:, :], pn, ACT.Copy), t_n, zs_free[g])
            ps.free[ni] = t_nc
            for j in range(4):
                t_b = mm(pz[:, j * 128:(j + 1) * 128], [(rb[g][:, j * 128:(j + 1) * 128], IDN[:, :])], [t_rb])
            rb_free[g] = t_b
            t_a = V.do(lambda e: e.tensor_tensor(at[:, g, :], zs[g][:, :], pz, ALU.mult), t_b, t_nc, kvt["at_v"])
            ps.free[zi] = t_a
            zs_free[g] = t_a
            return t_a

        def att_s(t_a):
            t_h = A.do(lambda e: e.activation(AH[:, :, :], at[:, :, :], ACT.Copy), t_a, kvt["oj"])
            t_l = G.do(lambda e: e.tensor_tensor(AL[:, :, :], at[:, :, :], r32(AH[:, :, :]), ALU.subtract), t_h)
            kvt["at_v"] = t_l
            return [t_h, t_l]

        def att_b(c, m, ts):
            sl = slice(c * 512, (c + 1) * 512)
            p, free, pi = ps.next()
            ms = slice(768 + m * 128, 768 + (m + 1) * 128)
            t_p = mm(p, [x for k in range(2) for x in three(W0H[:, k, ms], W0L[:, k, ms], AH[:, k, :], AL[:, k, :])], ts, free)
            kvt["oj"] = t_p
            t_x[c, m] = V.do(lambda e: e.scalar_tensor_tensor(X[:, m, sl], p, col("ob0", m), X[:, m, sl], ALU.add, ALU.add), t_p, t_x.get((c, m)))
            ps.free[pi] = t_x[c, m]

        def attention0():
            for tt in range(8):
                kv_in(tt)
                yield
                if tt >= 2:
                    kv_out(tt - 2)
                if tt % 4 == 3:
                    for m in range(2):
                        q_unit(tt // 4, m)
                        yield
            kv_out(6)
            kv_out(7)
            kv_sums()
            yield
            for c in (0, 1):
                att_a(c, 0)
                yield
                ts = att_s(att_a(c, 1))
                yield
                for tt in range(8 + 4 * c, 12 + 4 * c):
                    kv_in(tt)
                    yield
                    if tt > 9:
                        kv_out(tt - 2)
                for m in range(2):
                    att_b(c, m, ts)
                    yield
            kv_out(14)
            kv_out(15)
            q_unit(2, 0)
            yield
            kv_sums()
            q_unit(2, 1)
            yield
            for c in (2, 3):
                att_a(c, 0)
                yield
                ts = att_s(att_a(c, 1))
                yield
                for m in range(2):
                    if c == 2:
                        q_unit(3, m)
                    yield
                yield
                for m in range(2):
                    att_b(c, m, ts)
                    yield

        f_hs = Ring(hh)
        f_sg = Ring(sg)
        bank_free = [None, None]

        def ffn(c, gate_mm, up_mm, tokens, hidden, down, down_tokens, out):
            made = []

            def down_mm(m, sl, th, tl):
                for d in range(2):
                    t = mm(bank[6 + d], down(m, d, hh[sl][:, :], hl[sl][:, :]), [th, tl, *down_tokens],
                           bank_free[d] if m == 0 else None, start=(m == 0), stop=(m == 7))
                f_hs.free[sl] = t
                return t

            for m in range(8):
                pg, free, gi = pf.next()
                t_g = mm(pg, gate_mm(m, c), [*t_xn[c], *tokens], free)
                pu, free, ui = pf.next()
                t_u = mm(pu, up_mm(m, c), [], free)
                s, s_free, si = f_sg.next()
                _, h_free, hi = f_hs.next()
                t_h = hidden(m, s, s_free, pg, t_g, gi, pu, t_u, ui)
                t_hh = A.do(lambda e, s=s, hi=hi: e.activation(hh[hi][:, :], s[:, :], ACT.Copy), t_h, h_free)
                t_hl = G.do(lambda e, s=s, hi=hi: e.tensor_tensor(hl[hi][:, :], s[:, :], r32(hh[hi][:, :]), ALU.subtract), t_hh)
                f_sg.free[si] = t_hl
                made.append((m, hi, t_hh, t_hl))
                if m >= 3:
                    down_mm(*made[m - 3])
                yield
            down_mm(*made[5])
            down_mm(*made[6])
            t = down_mm(*made[7])
            for d in range(2):
                t_x[c, d] = bank_free[d] = out(d, c, t)
            yield

        def hidden0(m, s, s_free, pg, t_g, gi, pu, t_u, ui):
            t_s = A.do(lambda e: e.activation(s[:, :], pg, ACT.Tanh, scale=suh), t_g, s_free, tok["suh"])
            t_s = V.do(lambda e: e.scalar_tensor_tensor(s[:, :], s[:, :], 1.0, pg, ALU.add, ALU.mult), t_s)
            pf.free[gi] = t_s
            t_h = V.do(lambda e: e.tensor_tensor(s[:, :], s[:, :], pu, ALU.mult), t_u, t_s)
            pf.free[ui] = t_h
            return t_h

        def hidden1(m, s, s_free, pg, t_g, gi, pu, t_u, ui):
            t_s = A.do(lambda e: e.activation(s[:, :], pg, ACT.Silu, scale=col("wsg", m)), t_g, s_free)
            pf.free[gi] = t_s
            t_h = V.do(lambda e: e.scalar_tensor_tensor(s[:, :], pu, col("wsu", m), s[:, :], ALU.mult, ALU.mult), t_u, t_s)
            pf.free[ui] = t_h
            return t_h

        def wide(w_h, w_l, m0, c):
            sl = slice(c * 512, (c + 1) * 512)
            ms = slice(m0, m0 + 128)
            if w_l is None:
                return [x for k in range(2) for x in ((w_h[:, k, ms], XH[:, k, sl]), (w_h[:, k, ms], XL[:, k, sl]))]
            return [x for k in range(2) for x in three(w_h[:, k, ms], w_l[:, k, ms], XH[:, k, sl], XL[:, k, sl])]

        def out0(d, c, t):
            sl = slice(c * 512, (c + 1) * 512)
            return V.do(lambda e: e.scalar_tensor_tensor(X[:, d, sl], bank[6 + d], sgd, X[:, d, sl], ALU.mult, ALU.add), t, tok["sgd"], t_x.get((c, d)))

        w1_t, f1_t, fd_t = [], [], []
        done = {}

        def prep_attn1(i, t_w):
            for o, n, H, L in ((0, 768, W1H, W1L), (1536, 256, WOH, WOL)):
                raw = stg[i][:, o:o + 2 * n].rearrange("p (k n) -> p k n", k=2)
                t_h = A.do(lambda e, raw=raw, H=H: e.activation(H[:, :, :], raw, ACT.Copy), t_w, done["att0_pe"])
                t_l = G.do(lambda e, raw=raw, H=H, L=L: e.tensor_tensor(L[:, :, :], raw, r32(H[:, :, :]), ALU.subtract), t_h)
                w1_t.extend([t_h, t_l])
            st_free[i] = t_l

        def prep_ug(n, i, t_w):
            raw = stg[i][:, :].rearrange("p (k n) -> p k n", k=2)
            for k in range(2):
                for h in range(2):
                    p, free, pi = ps.next()
                    hs = slice(h * 512, (h + 1) * 512)
                    ds = slice(n * 1024 + h * 512, n * 1024 + (h + 1) * 512)
                    t_p = mm(p, [(HAD[:, :], raw[:, 0, hs]), ((HADN if k else HAD)[:, :], raw[:, 1, hs])], [t_w, t_hadn], free)
                    t_h = A.do(lambda e, p=p, k=k, ds=ds: e.activation(UGH[:, k, ds], p, ACT.Copy, scale=s16[:, 8 + k:9 + k]), t_p, t_sus, *done["att0"])
                    t_l = V.do(lambda e, p=p, k=k, ds=ds: e.scalar_tensor_tensor(UGL[:, k, ds], p, s16[:, 8 + k:9 + k], r32(UGH[:, k, ds]), ALU.mult, ALU.subtract), t_h)
                    ps.free[pi] = t_l
                    yield
            st_free[i] = t_p
            f1_t.extend([t_h, t_l])

        def butterflies(i, t_w):
            a, bf = stg[i][:, :], stg2
            t = t_w
            for s in (1, 2, 4):
                av, bv = (z.rearrange("p (o t i) -> p o t i", t=2, i=256 * s) for z in (a, bf))
                t = G.do(lambda e, av=av, bv=bv: e.tensor_tensor(bv[:, :, 0, :], av[:, :, 0, :], av[:, :, 1, :], ALU.add), t)
                yield
                t = G.do(lambda e, av=av, bv=bv: e.tensor_tensor(bv[:, :, 1, :], av[:, :, 0, :], av[:, :, 1, :], ALU.subtract))
                yield
                a, bf = bf, a
            st_free[i] = t
            tok["bf"] = t

        def prep_down():
            a, t = stg2, tok["bf"]
            for q in range(4):
                p, free, pi = ps.next()
                t_p = mm(p, [(HAD[:, :], a[:, q * 512:(q + 1) * 512])], [t, t_const], free)
                parts = [(2 * q + r, p[:, r * 256:(r + 1) * 256], s16b[:, 2 * q + r:2 * q + r + 1]) for r in range(2)]
                for cc, pr, sc in parts:
                    t_h = A.do(lambda e, cc=cc, pr=pr, sc=sc: e.activation(DH[:, cc, :], pr, ACT.Copy, scale=sc), t_p, t_sus, *done["att0"])
                for cc, pr, sc in parts:
                    t_l = V.do(lambda e, cc=cc, pr=pr, sc=sc: e.scalar_tensor_tensor(DL[:, cc, :], pr, sc, r32(DH[:, cc, :]), ALU.mult, ALU.subtract), t_h)
                ps.free[pi] = t_l
                yield
            ln_free[0] = ln_free[1] = t_p
            fd_t.extend([t_h, t_l])

        s16b = sb("s16b", 27.75, [128, 8])
        t_sus = V.do(lambda e: e.tensor_scalar(s16[:, 8:10], cols[:, COLS["suu"][0]:COLS["suu"][0] + 2], 1.0 / 16, None, ALU.mult), t_cols, t_const)
        t_sus = V.do(lambda e: e.tensor_scalar(s16b[:, :], cols[:, COLS["sud"][0]:COLS["sud"][0] + 8], 1.0 / 32, None, ALU.mult))
        t_hadn = V.do(lambda e: e.tensor_scalar(HADN[:, :], HAD[:, :], -1.0, None, ALU.mult))

        def ln1(c):
            return layernorm(c, [t_x[c, 0], t_x[c, 1]], T.last, c % 2, (c % 2) * 2, c % 2, ps)

        def ln1_pair(a, b):
            la, lb = ln1(a), ln1(b)
            next(la)
            yield
            next(lb)
            yield
            next(la)
            next(lb)
            yield
            yield
            next(la)
            yield
            next(lb)
            yield

        def scales():
            t = V.do(lambda e: e.tensor_tensor(sgd, sgt, sdn, ALU.mult), tern_t[2])
            t = V.do(lambda e: e.tensor_tensor(sgd, sgd, su, ALU.mult), t)
            tok["sgd"] = V.do(lambda e: e.tensor_scalar(sgd, sgd, 0.5, None, ALU.mult), t)

        def side0():
            for n, _ in enumerate(attention0()):
                if n == 10:
                    bf = butterflies(*loads[0])
                if n >= 10 and n % 3 == 1 and "bf" not in tok:
                    next(bf, None)
                    if "bf" in tok:
                        tok["ug0"] = stage(wf1[0], 2048)
                yield
            done["att0_pe"] = T.last()
            done["att0"] = [T.last(), V.last(), A.last(), G.last()]
            prep_attn1(*loads[1])
            ug1 = stage(wf1[1], 2048)
            yield
            yield from prep_down()
            yield from prep_ug(0, *tok["ug0"])
            yield from prep_ug(1, *ug1)
            yield from ln1_pair(0, 1)

        def main0():
            for c in range(NCH):
                yield from ffn(c, lambda m, c: wide(TU, None, m * 128, c), lambda m, c: wide(TG, None, m * 128, c),
                               [tern_t[0], tern_t[1]], hidden0,
                               lambda m, d, h, l: [(TD[:, m, d * 128:(d + 1) * 128], h), (TD[:, m, d * 128:(d + 1) * 128], l)],
                               [tern_t[2]], out0)

        sd0 = side0()
        next(sd0)
        next(tn[0])
        next(tn[1])
        tok["suh"] = V.do(lambda e: e.tensor_scalar(suh, su, 0.5, None, ALU.mult), tern_t[0])
        next(sd0)
        next(sd0)
        next(tn[1])
        next(tn[2])
        next(sd0)
        next(sd0)
        next(tn[2])
        scales()
        loads = [stage(wf1[2], 2048)]
        i, _ = stage(wa1, 1536)
        loads.append((i, d_st[i].start(S, stg[i][:, 1536:2048], wo1)))
        d_cs, d_pad = dsem("d_cs"), dsem("d_pad")
        for t, d in ((COS, cos_d), (SIN, sin_d)):
            t_cs = d_cs.start(S, t[:, :], d)
        t_pad = d_pad.start(S, scr_q[:, 48:64, :], pad_d[0:1].broadcast_to([16, 16, NT]))
        t_pad = d_pad.start(S, scr_k[:, 48:64, :], pad_d[1:2].broadcast_to([16, 16, NT]))
        for q in (A, V, G):
            q.wait(*[t for c in range(NCH) for t in t_xn[c]])
        weave(main0(), sd0, RATE0)
        run(sd0)
        t_ffn0_pe = T.last()
        t_ffn0_all = [T.last(), V.last(), A.last(), G.last()]

        rot_free = [None] * 4
        spl_free = [None] * 4
        d_sp = [dsem(f"d_sp{i}") for i in range(4)]

        def qk_unit(c, n):
            sl = slice(c * 512, (c + 1) * 512)
            cs = slice((c % 2) * 512, (c % 2 + 1) * 512)
            name, sc = ("qb1", 0.25) if n == 0 else ("kb1", 1.0)
            pp = []
            for m in range(2):
                p, free, pi = ps.next()
                pp.append((p, pi, mm(p, wide(W1H, W1L, n * 256 + m * 128, c), [*t_xn[c], *w1_t], free)))
            for m, (p, pi, t_p) in enumerate(pp):
                V.do(lambda e, p=p, m=m: e.scalar_tensor_tensor(rot[m][:, :], p, col(name, m), COS[:, cs], ALU.add, ALU.mult),
                     t_p, t_cs, rot_free[m], *t_ffn0_all)
                t = V.do(lambda e, p=p, m=m: e.scalar_tensor_tensor(rot[2 + m][:, :], p, col(name, m), SIN[:, cs], ALU.add, ALU.mult),
                         rot_free[3 - m], rot_free[2 + m])
                ps.free[pi] = t
            t_r = [G.do(lambda e: e.tensor_tensor(rot[0][:, :], rot[0][:, :], rot[3][:, :], ALU.subtract), t),
                   G.do(lambda e: e.tensor_tensor(rot[1][:, :], rot[1][:, :], rot[2][:, :], ALU.add))]
            rot_free[2] = rot_free[3] = t_r[1]
            for m in range(2):
                sh, sl_ = spl[2 * m], spl[2 * m + 1]
                t_h = A.do(lambda e, m=m, sh=sh: e.activation(sh[:, :], rot[m][:, :], ACT.Copy, scale=sc), t_r[m], spl_free[2 * m])
                t_l = V.do(lambda e, m=m, sh=sh, sl_=sl_: e.scalar_tensor_tensor(sl_[:, :], rot[m][:, :], sc, r32(sh[:, :]), ALU.mult, ALU.subtract),
                           t_h, spl_free[2 * m + 1])
                rot_free[m] = t_l
                dst = scr_q if n == 0 else scr_k
                for r in (0, 16 if n == 0 else 32):
                    spl_free[2 * m] = d_sp[2 * m].start(S, dst[:, r + 8 * m:r + 8 * m + 8, sl], sh[:, :], t_h)
                r = 32 if n == 0 else 16
                spl_free[2 * m + 1] = d_sp[2 * m + 1].start(S, dst[:, r + 8 * m:r + 8 * m + 8, sl], sl_[:, :], t_l)

        def v_unit(tt):
            tk = slice(tt * 128, (tt + 1) * 128)
            p, free, pi = ps.next()
            t_p = mm(p[:, 0:256], [x for k in range(2) for x in ((XH[:, k, tk], W1H[:, k, 512:768]), (XH[:, k, tk], W1L[:, k, 512:768]),
                                                                 (XL[:, k, tk], W1H[:, k, 512:768]))], [*t_xn[tt // 4]], free)
            ps.free[pi] = A.do(lambda e: e.activation(VV[:, tt, :, 0:16], p[:, 0:256].rearrange("p (h d) -> p h d", h=16), ACT.Copy), t_p, done["vv"])

        def out1(d, c, t):
            sl = slice(c * 512, (c + 1) * 512)
            return V.do(lambda e: e.scalar_tensor_tensor(X[:, d, sl], bank[6 + d], col("wsd", d), X[:, d, sl], ALU.mult, ALU.add), t)

        d_ks = [dsem(f"d_ks{i}") for i in range(3)]
        d_qs = [dsem(f"d_qs{i}") for i in range(4)]
        d_m = [dsem(f"d_m{i}") for i in range(2)]
        t_ki = [None] * 3
        t_qi = [None] * 4

        def init_slot(i, *tokens):
            for h in range(2):
                t_ki[i] = V.do(lambda e, h=h: e.memset(r32(KS[i][h][64 - 64 * h:128 - 64 * h, :]), 0.0), *tokens)

        k_tok = [None] * 16
        q_tok = [None] * 16

        def load(p, *tokens):
            b, j = divmod(p, 8)
            ts = slice(b * 1024, (b + 1) * 1024)
            S.wait(*spl_free, t_pad, *tokens)
            q_tok[p] = d_qs[p % 4].start(S, QS[p % 4][:, :], scr_q[2 * j:2 * j + 2, :, ts])
            for h in range(2):
                k_tok[p] = d_ks[p % 3].start(S, KS[p % 3][h][64 * h:64 * h + 64, :], scr_k[2 * j + h, :, ts])

        NP, LEAD, LAG = 16, 11, 2
        def main1():
            for c in range(NCH):
                yield from ffn(c, lambda m, c: wide(UGH, UGL, 1024 + m * 128, c), lambda m, c: wide(UGH, UGL, m * 128, c), f1_t, hidden1,
                               lambda m, d, h, l: [(DH[:, m, d * 128:(d + 1) * 128], h), (DH[:, m, d * 128:(d + 1) * 128], l),
                                                   (DL[:, m, d * 128:(d + 1) * 128], h)], fd_t, out1)

        def side1():
            init_slot(0, *t_ffn0_all)
            yield from ln1_pair(2, 3)
            for c in (0, 1):
                for n in range(2):
                    qk_unit(c, n)
                    yield
                    yield
            load(0, t_ffn0_all[0], *t_ffn0_all, *t_xn[3])
            done["vv"] = V.do(lambda e: e.memset(VV[:, :, :, 16:32], 1.0), *t_ffn0_all, *t_xn[3], *fd_t)
            tiles = iter(range(16))
            for tt in range(8):
                v_unit(tt)
                yield
            for c in (2, 3):
                for n in range(2):
                    qk_unit(c, n)
                    yield
                    for _ in range(2):
                        t_pe[0] = max_tile(0, next(tiles), ps)
                        yield
            for tt in range(8, 16):
                v_unit(tt)
                yield
                t_pe[0] = max_tile(0, next(tiles), ps)
                yield
            done["v_pe"], done["v_act"] = T.last(), A.last()
            init_slot(1)
            init_slot(2, *rot_free)
            for p in (1, 2):
                load(p, done["v_pe"], V.last(), G.last())
            max_rows(0, t_pe[0], ps)
            yield
            yield
            for ms in range(8, LEAD):
                for q in range(2):
                    t_pe[1] = max_tile(1, 2 * (ms % 8) + q, ps)
                    yield

        ST = Ring([4, 5, 6])
        mx_free = [None] * 2
        mrow_free = [None] * 2
        pv_free = None
        max_tok = [None] * NP
        m_tok = [None] * NP
        st_last = [None] * NP
        p_tok = {}
        p_free = [None] * 4
        oe_free = [None, None]
        t_pe = [None] * NP

        def max_tile(p, u, both=None):
            h, qt = divmod(u, 8)
            if both:
                i, free = 0, [both.next()[1] for _ in range(2)]
            else:
                i, free, mi = MX.next()
                free = [free]
            T.wait(*free, k_tok[p], q_tok[p], t_ki[p % 3])
            for half in range(2):
                f = lambda e, half=half: e.matmul(PS[:, i + half, :], QS[p % 4][:, qt * 128:(qt + 1) * 128],
                                                  KS[p % 3][h][:, half * 512:(half + 1) * 512], start=True, stop=True)
                if half == 0:
                    T.put(f)
                else:
                    t = T.do(f)
            max_tok[p] = V.do(lambda e: e.tensor_reduce(mx[p % 2][:, u:u + 1], PS[:, i:i + 2, :], AX.XY, ALU.max), t,
                               mx_free[p % 2] if u == 0 else None)
            if both:
                both.free = [max_tok[p]] * 2
            else:
                MX.free[mi] = max_tok[p]
            return t

        def max_rows(p, t_pe, ring):
            o, free, si = ring.next()
            if ring is ST:
                o = bank[o]
            t = T.do(lambda e: e.transpose(o[0:16, 0:128], mx[p % 2][:, :], IDN[:, :]), free, max_tok[p])
            mx_free[p % 2] = t
            t = A.do(lambda e: e.activation(mrow[p % 2][:, :], o[0:16, 0:128], ACT.Copy, scale=-1.0), t, mrow_free[p % 2])
            ring.free[si] = t
            m_tok[p] = d_m[p % 2].start(S, QS[p % 4][48:113:64, :].rearrange("a (q n) -> a q n", q=8), mrow[p % 2][:, :], t, t_pe)
            mrow_free[p % 2] = m_tok[p]

        def scores(s, c):
            p, kt = divmod(s, 8)
            h, half = divmod(c, 2)
            i, free, si = ST.next()
            t = T.do(lambda e: e.matmul(PS[:, i, :], KS[p % 3][h][:, kt * 128:(kt + 1) * 128], QS[p % 4][:, half * 512:(half + 1) * 512],
                                        start=True, stop=True), free, m_tok[p])
            st_last[p] = t
            ST.free[si] = A.do(lambda e: e.activation(P[s % 4][:, c * 512:(c + 1) * 512], PS[:, i, :], ACT.Exp), t, p_free[s % 4] if c == 0 else None)
            p_tok[s] = ST.free[si]

        def values(s):
            nonlocal pv_free
            p, kt = divmod(s, 8)
            b, j = divmod(p, 8)
            T.wait(p_tok[s], done["v_act"], pv_free if kt == 0 else None)
            for c in range(4):
                f = lambda e, c=c: e.matmul(PS[32 * c:32 * c + 32, 7, :], VV[:, 8 * b + kt, 2 * j + c // 2, :], P[s % 4][:, c * 512:(c + 1) * 512],
                                            start=(kt == 0), stop=(kt == 7), tile_position=(0, 32 * c))
                if c < 3:
                    T.put(f)
                else:
                    t = T.do(f)
            p_free[s % 4] = t
            if p == NP - 1 and kt == 7:
                last_pair(t)
            elif kt == 7:
                o = p % 2
                g = p // 4
                pv_free = A.do(lambda e: e.activation(OE[o][:, :], PS[:, 7, :], ACT.Copy), t, oe_free[o])
                t = d_oe[o].start(G, scr_o[p].rearrange("c k n -> (c k) n"), OE[o][:, :], pv_free)
                oe_free[o] = t
                for h in range(2):
                    row = 32 * (p % 4) + 16 * h
                    d_num[g % 2].start(G, NUM[g % 2][row:row + 16, :].rearrange("r (a n) -> r a n", a=2),
                                       scr_o[p, 2 * h:2 * h + 2, 0:16, :].rearrange("a r n -> r a n"), t, num_free[g % 2], t_ffn1_pe)
                t = d_rc[o].start(G, RC[o][:, :], scr_o[p, :, 16, :].rearrange("c (q n) -> c q n", n=16), rc_free[o])
                later(now[0] + 4 if p < 14 else now[0] + 2, lambda: recip(p, t))

        def last_pair(t_pv):
            t_o = A.do(lambda e: e.activation(OE[1][:, :], PS[:, 7, :], ACT.Copy), t_pv, oe_free[1])
            t_r = V.do(lambda e: e.reciprocal(OE[0][:, :], OE[1][:, :]), t_o, oe_free[0])
            for c in range(4):
                h, half = divmod(c, 2)
                row = 96 + 16 * h
                d_last.start(S, NUM[1][row:row + 16, half * 512:(half + 1) * 512], OE[1][32 * c:32 * c + 16, :], t_o, num_free[1])
            for c in range(4):
                h, half = divmod(c, 2)
                row = 96 + 16 * h
                d_last.start(S, DEN[1][row:row + 16, half * 512:(half + 1) * 512], OE[0][32 * c + 16:32 * c + 32, :], t_r)
            later(now[0] + 1, lambda: group(3))

        def recip(p, t_in):
            o, g = p % 2, p // 4
            t = V.do(lambda e: e.reciprocal(RC[o][:, :], RC[o][:, :]), t_in)
            t = d_rs[o].start(G, scr_r[p].rearrange("c (q n) -> (c q) n", n=16), RC[o][:, :], t)
            rc_free[o] = t
            for h in range(2):
                row = 32 * (p % 4) + 16 * h
                d_num[g % 2].start(G, DEN[g % 2][row:row + 16, :].rearrange("r (a n) -> r a n", a=2),
                                   scr_r[p, 2 * h:2 * h + 2, :].rearrange("(o a) n -> o a n", o=1).broadcast_to([16, 2, 512]), t, num_free[g % 2])
            if p % 4 == 3:
                later(now[0] + 4, lambda: group(g))

        def group(g):
            i = g % 2
            b, f = divmod(g, 2)
            t_n = (G if g < 3 else V).do(lambda e: e.tensor_tensor(NUM[i][:, :], NUM[i][:, :], DEN[i][:, :], ALU.mult), (d_num[i].sem, d_num[i].n), (d_last.sem, d_last.n))
            t_h = A.do(lambda e: e.activation(OH[i][:, :], NUM[i][:, :], ACT.Identity, bias=col("vb1", f)), t_n, oh_free[i])
            t_l = V.do(lambda e: e.scalar_tensor_tensor(OL[i][:, :], NUM[i][:, :], col("vb1", f), r32(OH[i][:, :]), ALU.add, ALU.subtract), t_h)
            num_free[i] = t_l
            for n in range(4):
                if g < 3:
                    later(now[0] + 1 + n, lambda n=n: project(g, n, [t_h, t_l]))
                else:
                    project(g, n, [t_h, t_l])

        def project(g, n, ts):
            i = g % 2
            b, f = divmod(g, 2)
            cc, m = divmod(n, 2)
            hs = slice(cc * 512, (cc + 1) * 512)
            sl = slice((2 * b + cc) * 512, (2 * b + cc + 1) * 512)
            ms = slice(m * 128, (m + 1) * 128)
            k, free, si = ST.next()
            t_p = mm(PS[:, k, :], three(WOH[:, f, ms], WOL[:, f, ms], OH[i][:, hs], OL[i][:, hs]), ts, free)
            oh_free[i] = t_p
            if f == 0:
                t_o = V.do(lambda e: e.scalar_tensor_tensor(X[:, m, sl], PS[:, k, :], col("ob1", m), X[:, m, sl], ALU.add, ALU.add), t_p)
            else:
                t_o = V.do(lambda e: e.tensor_tensor(X[:, m, sl], PS[:, k, :], X[:, m, sl], ALU.add), t_p, t_x[2 * b + cc, m])
            t_x[2 * b + cc, m] = t_o
            ST.free[si] = t_o
            if f == 1:
                d_y.start(S, yT[:, m, sl], X[:, m, sl], t_o)

        d_y = dsem("d_y")
        d_oe = [dsem(f"d_oo{i}") for i in range(2)]
        d_num = [dsem(f"d_num{i}") for i in range(2)]
        d_last = dsem("d_last")
        d_rc = [dsem(f"d_rc{i}") for i in range(2)]
        d_rs = [dsem(f"d_rs{i}") for i in range(2)]
        num_free, rc_free, oh_free = [None] * 2, [None] * 2, [None] * 2
        plan = {}
        now = [0]

        def later(s, f):
            plan.setdefault(s, []).append(f)

        f_free = pf.free
        pf = Ring(bank[2:6])
        pf.free = [kvt["kv_free"], *f_free]
        sd1 = side1()
        weave(main1(), sd1, RATE1)
        run(sd1)
        t_ffn1_pe = T.last()
        t_end = [V.last(), A.last()]
        MX = Ring([0, 2])
        MX.free = [V.last(), V.last()]
        ST.free = [V.last()] * 3
        T.wait(*t_end, G.last())
        for q in (A, V):
            q.wait(t_ffn1_pe)
        A.wait(V.last(), G.last())
        s = 0
        while s < 8 * NP + LAG or any(k >= s for k in plan):
            now[0] = s
            ms = s + LEAD
            live = s < 8 * NP
            maxing = ms < 8 * NP
            if 2 <= ms // 8 <= NP and ms % 8 == 0:
                max_rows(ms // 8 - 1, t_pe[ms // 8 - 1], ST)
            for f in plan.get(s, []):
                f()
            for q in range(2):
                if live:
                    scores(s, 2 * q)
                if maxing:
                    t_pe[ms // 8] = max_tile(ms // 8, 2 * (ms % 8) + q)
                if live:
                    scores(s, 2 * q + 1)
            if 0 <= s - LAG < 8 * NP:
                values(s - LAG)
            if live and s % 8 == 7 and s // 8 + 3 < NP:
                load(s // 8 + 3, st_last[s // 8])
            s += 1
        S.wait((d_y.sem, d_y.n))

        block = ctx.enter_context(nc.Block())

        @block.sync
        def _(e):
            S.run(e)

        @block.scalar
        def _(e):
            A.run(e)

        @block.vector
        def _(e):
            V.run(e)

        @block.gpsimd
        def _(e):
            G.run(e)

        @block.tensor
        def _(e):
            T.run(e)


def hadamard(n):
    import numpy as np
    h = np.ones((1, 1), np.float32)
    while h.shape[0] < n:
        h = np.block([[h, h], [h, -h]])
    return np.ascontiguousarray(h, np.float32)


def kernel(**inp):
    import numpy as np
    import concourse.bacc as bacc
    from concourse.bass_utils import run_bass_kernel_spmd as run

    inp = {k: np.asarray(v) for k, v in inp.items()}

    def fold(w):
        n, d = w.shape
        return w.T.reshape(d // 128, 128, n).transpose(1, 0, 2)

    def flat(w):
        return np.ascontiguousarray(w.reshape(128, -1))

    half = np.arange(256).reshape(16, 2, 8).transpose(1, 0, 2).reshape(-1)
    x = inp["L0_attn_hidden_states"]
    xT = np.ascontiguousarray(fold(x.reshape(NT, 256)))
    wa0 = flat(np.concatenate([fold(inp[f"L0_attn_{n}_w"]) for n in "qkvo"], axis=2))
    tern = [flat(fold(inp[f"L0_ffn_W_{n}"])) for n in ("up", "gate", "down")]
    q, k, v = (inp[f"L1_attn_{n}_w"] for n in "qkv")
    wa1 = flat(fold(np.concatenate([q[half], k[half], v], axis=0)))
    wo1 = flat(fold(inp["L1_attn_out_w"]))
    wf1 = [flat(fold(inp[f"L1_ffn_W_{n}"])) for n in ("up", "gate", "down")]

    def cut(a):
        return a.reshape(-1, 128).T

    qb, kb = inp["L1_attn_q_b"], inp["L1_attn_k_b"]
    ws = inp["L1_ffn_Wscale_ug"]
    part = np.arange(128)
    cols = np.ascontiguousarray(np.concatenate([
        cut(inp["L0_attn_q_b"]), cut(inp["L0_attn_o_b"]), cut(qb[half]), cut(qb[half]), cut(kb[half]), cut(kb[half]),
        cut(inp["L1_attn_v_b"]), cut(inp["L1_attn_out_b"]), cut(inp["L1_ffn_SU_ug"]), cut(inp["L1_ffn_SU_dp"]),
        cut(ws[:1024]), cut(ws[1024:]), cut(inp["L1_ffn_Wscale_dp"]),
        (part == 48).astype(np.float32)[:, None], (part == 112).astype(np.float32)[:, None],
        np.full((128, 1), 1e-6, np.float32), np.full((128, 1), 1e-5, np.float32)], axis=1))
    bkv = np.ascontiguousarray(np.broadcast_to(np.concatenate([inp["L0_attn_k_b"], inp["L0_attn_v_b"]])[None, :], (128, 512)))
    inv = (1.0 / np.float32(10000.0) ** (np.arange(0, 16, 2, dtype=np.float32) / np.float32(16))).astype(np.float32)
    fr = np.arange(1024, dtype=np.float32)[:, None] * inv[None, :]
    cos = np.ascontiguousarray(np.tile(np.cos(fr).T, (16, 1)).astype(np.float32))
    sin = np.ascontiguousarray(np.tile(np.sin(fr).T, (16, 1)).astype(np.float32))
    mask = (part[:, None] // 16 == part[None, :] // 16).astype(np.float32)
    arrays = dict(xT=xT, wa0=wa0, wa1=wa1, wo1=wo1, cols=cols, bkv=bkv, cos=cos, sin=sin, had=hadamard(128),
                  mask=mask, ident=np.eye(128, dtype=np.float32))
    pad = np.zeros((2, 16, NT), np.float32)
    pad[1, 0] = 1.0
    arrays["pad"] = pad
    for i in range(3):
        arrays[f"tern{i}"] = tern[i]
        arrays[f"wf1{i}"] = wf1[i]
    arrays = {f"in_{n}": a for n, a in arrays.items()}

    nc = bacc.Bacc("TRN2", target_bir_lowering=False, num_devices=1)
    t = {n: nc.dram_tensor(n, a.shape, F32, kind="ExternalInput").ap() for n, a in arrays.items()}
    y = nc.dram_tensor("out_y", (128, 2, NT), F32, kind="ExternalOutput").ap()
    program(nc, t["in_xT"], t["in_wa0"], [t[f"in_tern{i}"] for i in range(3)], t["in_wa1"], t["in_wo1"],
            [t[f"in_wf1{i}"] for i in range(3)], t["in_cols"], t["in_bkv"], t["in_cos"], t["in_sin"], t["in_had"], t["in_mask"],
            t["in_ident"], t["in_pad"], y)
    r = run(nc, [arrays], core_ids=[0])
    out = np.asarray(r.results[0]["out_y"])
    return np.ascontiguousarray(out.transpose(2, 1, 0).reshape(2, 1024, 256))
```

```python
from contextlib import ExitStack
from itertools import chain

import concourse.bass as bass
from concourse import mybir

F32 = mybir.dt.float32
F32R = mybir.dt.float32r
ALU = mybir.AluOpType
ACT = mybir.ActivationFunctionType
AX = mybir.AxisListType

NT = 2048
NCH = 4
KB = 1024

FIRST = 12
RATE0 = 1.65
RATE1 = 1.7

COLS = dict(qb0=(0, 2), ob0=(2, 2), qb1=(4, 2), kb1=(8, 2), vb1=(12, 2), ob1=(14, 2),
            suu=(16, 2), sud=(18, 8), wsu=(26, 8), wsg=(34, 8), wsd=(42, 2), rowa=(44, 1), rowb=(45, 1), eps=(46, 1), eps5=(47, 1))
NCOL = 48


class Queue:

    def __init__(self, sem):
        self.sem, self.n, self.ops, self.seen = sem, 0, [], {}

    def wait(self, *tokens):
        for t in tokens:
            if t is None:
                continue
            sem, v = t
            if self.seen.get(sem.name, 0) < v:
                self.seen[sem.name] = v
                self.ops.append(lambda e, sem=sem, v=v: e.wait_ge(sem, v))

    def do(self, f, *tokens):
        self.wait(*tokens)
        self.n += 1
        self.ops.append(lambda e: f(e).then_inc(self.sem, 1))
        return self.sem, self.n

    def put(self, f, *tokens):
        self.wait(*tokens)
        self.ops.append(f)

    def fill(self, out, value, *tokens):
        self.wait(self.last())
        t = self.do(lambda e: e.memset(out, value), *tokens)
        self.wait(t)
        return t

    def last(self):
        return (self.sem, self.n) if self.n else None

    def run(self, e):
        for f in self.ops:
            f(e)


class Arrivals:

    def __init__(self, sem):
        self.sem, self.n = sem, 0

    def start(self, q, out, in_, *tokens):
        self.n += 16
        out, in_ = (a.bitcast(F32) if a.dtype == F32R else a for a in (out, in_))
        q.put(lambda e: e.dma_start(out, in_).then_inc(self.sem, 16), *tokens)
        return self.sem, self.n


class Ring:

    def __init__(self, slots):
        self.slots, self.free, self.i = slots, [None] * len(slots), -1

    def next(self):
        self.i = (self.i + 1) % len(self.slots)
        return self.slots[self.i], self.free[self.i], self.i


def program(nc, xT, wa0, tern, wa1, wo1, wf1, cols_d, bkv_d, cos_d, sin_d, had_d, mask_d, ident_d, pad_d, sel_d, wl_d, yT):
    with ExitStack() as ctx:
        def sem(name):
            return ctx.enter_context(nc.semaphore(name))

        base = -(-nc.sbuf_base // 32) * 32

        def sb(name, kb, shape, dt=F32):
            return nc.alloc_sbuf_tensor_at(name, shape, dt, offset=base + int(kb * KB))

        V, A, G, T, S = (Queue(sem(n)) for n in ("s_dve", "s_act", "s_pool", "s_pe", "s_sp"))

        def dsem(name):
            return Arrivals(sem(name))

        X = sb("X", 0, [128, 2, NT])
        COS = sb("COS", 16, [128, 1024])
        SIN = sb("SIN", 20, [128, 1024])
        cols = sb("cols", 24, [128, NCOL])
        s16 = sb("s16", 24.25, [128, 16])
        HAD = sb("HAD", 24.5, [128, 128])
        HADN = sb("HADN", 25, [128, 128])
        IDN = sb("IDN", 25.5, [128, 128])
        MASK = sb("MASK", 26, [128, 128])
        MEAN = sb("MEAN", 26.5, [128, 128])
        ONES = sb("ONES", 27, [128, 128])
        mx = [sb(f"mx{i}", 27.5 + i / 16, [128, 16]) for i in range(2)]
        mrow = [sb(f"mrow{i}", 206 + i / 2, [16, 128], F32R) for i in range(2)]
        XH = sb("XH", 28, [128, 2, NT], F32R)
        XL = sb("XL", 44, [128, 2, NT], F32R)
        W0H = sb("W0H", 60, [128, 2, 1024], F32R)
        W0L = sb("W0L", 68, [128, 2, 1024], F32R)
        W1H = sb("W1H", 60, [128, 2, 768], F32R)
        W1L = sb("W1L", 66, [128, 2, 768], F32R)
        WOH = sb("WOH", 80, [128, 2, 256], F32R)
        WOL = sb("WOL", 82, [128, 2, 256], F32R)
        TU = sb("TU", 84, [128, 2, 1024], F32R)
        TG = sb("TG", 92, [128, 2, 1024], F32R)
        TD = sb("TD", 100, [128, 8, 256], F32R)
        QP = sb("QP", 108, [128, 2, NT])
        zk = [sb(f"zk{i}", 124 + i, [128, 256]) for i in range(4)]
        ek = [sb(f"ek{i}", 128 + i, [128, 256]) for i in range(4)]
        ve = [sb(f"ve{i}", 132 + 1.25 * i, [128, 2, 129]) for i in range(4)]
        kvb = [sb(f"kvb{i}", 137 + i / 2, [128, 128]) for i in range(2)]
        zb = [sb(f"zb{i}", 138 + i / 2, [128, 8]) for i in range(2)]
        zs = [sb(f"zs{i}", 139 + 2 * i, [128, 512]) for i in range(2)]
        at = sb("at", 143, [128, 2, 512])
        AH = sb("AH", 147, [128, 2, 512], F32R)
        AL = sb("AL", 151, [128, 2, 512], F32R)
        BKV = sb("BKV", 204, [128, 512])
        UGH = sb("UGH", 108, [128, 2, 2048], F32R)
        UGL = sb("UGL", 124, [128, 2, 2048], F32R)
        DH = sb("DH", 140, [128, 8, 256], F32R)
        DL = sb("DL", 148, [128, 8, 256], F32R)
        hh = [sb(f"hh{i}", (156, 158, 160, 76)[i], [128, 512], F32R) for i in range(4)]
        hl = [sb(f"hl{i}", (162, 164, 166, 78)[i], [128, 512], F32R) for i in range(4)]
        sg = [sb(f"sg{i}", 168 + 2 * i, [128, 512]) for i in range(3)]
        stg = [sb(f"stg{i}", 174 + 8 * i, [128, 2048]) for i in range(2)]
        XC = [sb(f"XC{i}", (190, 194, 156, 160)[i], [128, 2, 512]) for i in range(4)]
        SQ = [sb(f"SQ{i}", (198, 164, 72)[i], [128, 2, 512]) for i in range(3)]
        rb = [sb(f"rb{i}", 198 + 2 * i, [128, 512]) for i in range(2)]
        stg2 = sb("stg2", 190, [128, 2048])[:, :]
        rstd = [sb(f"rstd{i}", 202 + i / 32, [128, 4]) for i in range(4)]
        rz = [sb(f"rz{i}", 202.5 + i / 8, [128, 32]) for i in range(2)]
        rot = [sb(f"rot{i}", 84 + 2 * i, [128, 512]) for i in range(4)]
        spl = [sb(f"spl{i}", 92 + 2 * i, [128, 512], F32R) for i in range(4)]
        VV = sb("VV", 174, [128, 16, 16, 32])
        KS = [[sb(f"KS{i}{h}", (100, 16, 84)[i] + 4 * h, [128, 1024], F32R) for h in range(2)] for i in range(3)]
        QS = [sb(f"QS{i}", (72, 60, 64, 68)[i], [128, 1024], F32R) for i in range(4)]
        P = [sb(f"P{i}", 108 + 8 * i, [128, 2048]) for i in range(4)]
        OE = [sb(f"OE{i}", 140 + 2 * i, [128, 512]) for i in range(2)]
        NUM = [sb(f"NUM{i}", 28 + 4 * i, [128, 1024]) for i in range(2)]
        DEN = [sb(f"DEN{i}", 36 + 4 * i, [128, 1024]) for i in range(2)]
        OH = [sb(f"OH{i}", 44 + 4 * i, [128, 1024], F32R) for i in range(2)]
        OL = [sb(f"OL{i}", 52 + 4 * i, [128, 1024], F32R) for i in range(2)]
        SEL = sb("SEL", 146, [128, 128])
        WLR = sb("WLR", 144, [128, 2, 256])
        WLH = sb("WLH", 76, [128, 2, 256], F32R)
        WLL = sb("WLL", 78, [128, 2, 256], F32R)
        LH = sb("LH", 152, [128, 512], F32R)
        LL = sb("LL", 154, [128, 512], F32R)
        RC = [sb(f"RC{i}", 150 + i / 8, [128, 16]) for i in range(2)]
        PS = ctx.enter_context(nc.psum_tensor("PS", [128, 8, 512], F32))
        bank = [PS[:, i, :] for i in range(8)]
        scr_q, scr_k = (nc.dram_tensor(n, (16, 64, NT), F32).ap() for n in ("scr_q", "scr_k"))
        scr_o = nc.dram_tensor("scr_o", (16, 4, 32, 512), F32).ap()
        scr_r = nc.dram_tensor("scr_r", (16, 4, 512), F32).ap()

        def col(name, i=0):
            a = COLS[name][0] + i
            return cols[:, a:a + 1]

        def r32(ap):
            return ap.bitcast(F32)

        d_c = dsem("d_c")
        d_x = [dsem(f"d_x{c}") for c in range(NCH)]
        d_st = [dsem(f"d_st{i}") for i in range(2)]
        d_cols = dsem("d_cols")
        t_cols = d_cols.start(A, cols[:, :], cols_d)
        for c in range(NCH):
            t_x = d_x[c].start(S, X[:, :, c * 512:(c + 1) * 512], xT[:, :, c * 512:(c + 1) * 512])
        for t, d in ((IDN, ident_d), (MASK, mask_d), (HAD, had_d)):
            t_const = d_c.start(A, t[:, :], d)
        t_const = d_c.start(A, BKV[:, :], bkv_d)

        t_mean = V.do(lambda e: e.memset(MEAN[:, :], 1.0 / 256))
        t_ones = V.do(lambda e: e.memset(ONES[:, :], 1.0))
        for i in range(4):
            t_ve1 = V.do(lambda e, i=i: e.memset(ve[i][:, :, 128:129], 1.0))

        ps = Ring(bank[0:2])
        pf = Ring(bank[3:6])

        st_free = [None, None]
        st_n = [0]

        def stage(src, n):
            i = st_n[0] % 2
            st_n[0] += 1
            t = d_st[i].start(S, stg[i][:, 0:n], src, st_free[i])
            return i, t


        def mm(out, pairs, tokens, free=None, start=True, stop=True):
            T.wait(free, *tokens)
            for j, (l, r) in enumerate(pairs):
                f = lambda e, l=l, r=r, j=j: e.matmul(out, l, r, start=start and j == 0, stop=stop and j == len(pairs) - 1)
                if j == len(pairs) - 1:
                    return T.do(f)
                T.put(f)

        def three(wh, wl, xh, xl):
            return [(wh, xh), (wh, xl), (wl, xh)]

        t_xn = {}
        t_x = {}
        mm(bank[7][:, 0:128], [(MEAN[:, :], MEAN[:, :])] * 8, [t_mean])
        ln_free = [None] * 4
        sq_free = [None] * 3
        rstd_free = [None] * 4

        def layernorm(c, t_in, t_free, xi, qi, ri, ring):
            sl = slice(c * 512, (c + 1) * 512)
            xc, sq, rs = XC[xi], SQ[qi], rstd[ri]
            m, free, i = ps.next()
            t_m = mm(m, [(MEAN[:, :], X[:, k, sl]) for k in range(2)], [t_mean, *t_in], free)
            for k in range(2):
                t_xc = V.do(lambda e, k=k: e.tensor_tensor(xc[:, k, :], X[:, k, sl], m, ALU.subtract), t_m, ln_free[xi])
            ps.free[i] = t_xc
            t_sq = A.do(lambda e: e.activation(sq[:, :, :], xc[:, :, :], ACT.Square), t_xc, sq_free[qi])
            yield
            v, free, i = ring.next()
            for j in range(4):
                t_v = mm(v[:, j:j + 1], [(sq[:, k, j * 128:(j + 1) * 128], MEAN[:, 0:1]) for k in range(2)], [t_sq], free)
            sq_free[qi] = t_v
            t_sd = A.do(lambda e, v=v: e.activation(rs[:, :], v[:, 0:4], ACT.Sqrt, bias=col("eps5")), t_v, t_cols, rstd_free[ri])
            ring.free[i] = t_sd
            t_r = V.do(lambda e: e.reciprocal(rs[:, :], rs[:, :]), t_sd)
            yield
            w, free, i = ring.next()
            for j in range(4):
                t_b = mm(w[:, j * 128:(j + 1) * 128], [(rs[:, j:j + 1].broadcast_to([128, 128]), IDN[:, :])], [t_r, t_const], free)
            rstd_free[ri] = t_b
            for k in range(2):
                t_n = V.do(lambda e, k=k: e.tensor_tensor(xc[:, k, :], xc[:, k, :], w, ALU.mult), t_b)
            ring.free[i] = t_n
            t_h = A.do(lambda e: e.activation(XH[:, :, sl], xc[:, :, :], ACT.Copy), t_n, t_free())
            t_l = G.do(lambda e: e.tensor_tensor(XL[:, :, sl], xc[:, :, :], r32(XH[:, :, sl]), ALU.subtract), t_h)
            ln_free[xi] = t_l
            t_xn[c] = [t_h, t_l]
            yield

        def run(g):
            for _ in g:
                pass

        def weave(main, side, rate):
            due = 0.0
            for _ in main:
                due += rate
                while due >= 1:
                    due -= 1
                    next(side, None)

        tern_t = {}

        def ternary(n, dst):
            i, t_w = stage(tern[n], 2048)
            flat = dst[:, :, :].rearrange("p k n -> p (k n)")
            t_a = A.do(lambda e: e.activation(flat, stg[i][:, :], ACT.Abs, accum_out=s16[:, n:n + 1]), t_w)
            yield
            p, free, pi = ps.next()
            t_s = mm(p[:, 0:1], [(ONES[:, :], s16[:, n:n + 1])], [t_a, t_ones], free)
            sc, hi, lo = (s16[:, j + n:j + n + 1] for j in (3, 10, 13))
            t_sc = V.do(lambda e: e.tensor_scalar(sc, p[:, 0:1], 1.0 / 262144, 1e-8, ALU.mult, ALU.add), t_s)
            ps.free[pi] = t_sc
            t_hi = V.do(lambda e: e.tensor_scalar(hi, sc, 0.5, None, ALU.mult), t_sc)
            t_lo = V.do(lambda e: e.tensor_scalar(lo, sc, -0.5, None, ALU.mult))
            t_p = V.do(lambda e: e.tensor_scalar(flat, stg[i][:, :], lo, None, ALU.is_lt), t_lo, t_w)
            yield
            for j in range(2):
                js = slice(j * 1024, (j + 1) * 1024)
                t_t = V.do(lambda e, js=js: e.scalar_tensor_tensor(flat[:, js], stg[i][:, js], hi, r32(flat[:, js]), ALU.is_gt, ALU.subtract), t_p)
                if j == 0:
                    yield
            st_free[i] = t_t
            tern_t[n] = t_t
            yield

        ln0 = [layernorm(c, [(d_x[c].sem, d_x[c].n)], lambda: None, c, c % 2, c, pf) for c in range(NCH)]
        wi, t_w = stage(wa0, 2048)
        raw0 = stg[wi][:, :].rearrange("p (k n) -> p k n", k=2)
        tn = chain(*(ternary(n, t) for n, t in enumerate((TU, TG, TD))))
        for i in (0, 1, 0, 2, 1):
            next(ln0[i])
        t_wh = A.do(lambda e: e.activation(W0H[:, :, :], raw0, ACT.Copy), t_w)
        for i in (3, 2):
            next(ln0[i])
        t_wl = V.do(lambda e: e.tensor_tensor(W0L[:, :, :], raw0, r32(W0H[:, :, :]), ALU.subtract), t_wh)
        st_free[wi] = t_wl
        t_w0 = [t_wh, t_wl]
        for i in (0, 3, 1):
            next(ln0[i])
        su, sgt, sdn, sgd, suh = (s16[:, i:i + 1] for i in (3, 4, 5, 6, 7))
        tok = {}

        zs_free = [None, None]
        rz_free, rb_free = [None, None], [None, None]
        q_t = {}
        kv_bank = bank[2]
        kvt = {"kv_free": None, "ve": [None] * 4, "at": [None, None], "at_v": None, "oj": None, "b": None}
        kin = {}

        def q_unit(c, m):
            sl = slice(c * 512, (c + 1) * 512)
            p, free, pi = ps.next()
            ms = slice(m * 128, (m + 1) * 128)
            t_p = mm(p, [x for k in range(2) for x in three(W0H[:, k, ms], W0L[:, k, ms], XH[:, k, sl], XL[:, k, sl])],
                     [*t_xn[c], *t_w0], free)
            t_n = V.do(lambda e: e.tensor_scalar(zs[m][:, :], p, col("qb0", m), 0.0, ALU.add, ALU.min), t_p, t_const, zs_free[m])
            t_r = V.do(lambda e: e.tensor_scalar(QP[:, m, sl], p, col("qb0", m), 0.0, ALU.add, ALU.max))
            ps.free[pi] = t_r
            t_e = A.do(lambda e: e.activation(zs[m][:, :], zs[m][:, :], ACT.Exp), t_n)
            q_t[c, m] = G.do(lambda e: e.tensor_tensor(QP[:, m, sl], zs[m][:, :], QP[:, m, sl], ALU.add), t_r, t_e)
            zs_free[m] = q_t[c, m]

        def kv_in(tt):
            j = tt % 4
            tk = slice(tt * 128, (tt + 1) * 128)
            p, free, pi = ps.next()
            t_p = mm(p, [x for k in range(2) for x in ((XH[:, k, tk], W0H[:, k, 256:768]), (XH[:, k, tk], W0L[:, k, 256:768]),
                                                       (XL[:, k, tk], W0H[:, k, 256:768]))], [*t_xn[tt // 4], *t_w0], free)
            t_z = V.do(lambda e: e.tensor_tensor(zk[j][:, :], p[:, 0:256], BKV[:, 0:256], ALU.add), t_p, t_const, kvt["ve"][j])
            t_v = V.do(lambda e: e.tensor_tensor(ve[j][:, :, 0:128], p[:, 256:512].rearrange("p (g n) -> p g n", g=2),
                                                 BKV[:, 256:512].rearrange("p (g n) -> p g n", g=2), ALU.add))
            ps.free[pi] = t_v
            t_m = G.do(lambda e: e.tensor_scalar(ek[j][:, :], zk[j][:, :], 0.0, None, ALU.min), t_z)
            t_e = A.do(lambda e: e.activation(ek[j][:, :], ek[j][:, :], ACT.Exp), t_m)
            t_r = G.do(lambda e: e.tensor_scalar(zk[j][:, :], zk[j][:, :], 0.0, None, ALU.max))
            t_k = G.do(lambda e: e.tensor_tensor(zk[j][:, :], ek[j][:, :], zk[j][:, :], ALU.add), t_e, t_r)
            kin[tt] = (t_k, t_v)

        def kv_out(tt):
            j, i = tt % 4, tt % 8
            T.wait(*kin[tt], t_ve1, kvt["kv_free"] if i == 0 else None)
            for g in range(2):
                f = lambda e, g=g: e.matmul(kv_bank[:, g * 129:(g + 1) * 129], zk[j][:, g * 128:(g + 1) * 128], ve[j][:, g, :],
                                            start=(i == 0 and g == 0), stop=(i == 7), skip_group_check=True)
                if g == 0:
                    T.put(f)
                else:
                    kvt["ve"][j] = T.do(f)

        def kv_sums():
            t = kvt["ve"][3]
            V.wait(t, *kvt["at"])
            for g in range(2):
                V.do(lambda e, g=g: e.tensor_tensor(kvb[g][:, :], kv_bank[:, g * 129:g * 129 + 128], MASK[:, :], ALU.mult))
                t = V.do(lambda e, g=g: e.tensor_scalar(zb[g][:, :], MASK[:, 0:128:16], kv_bank[:, g * 129 + 128:g * 129 + 129], None, ALU.mult))
            kvt["kv_free"] = kvt["b"] = t

        def att_z(c, g):
            if g:
                ps.next()
            sl = slice(c * 512, (c + 1) * 512)
            pz, z_free, zi = ps.next()
            for j in range(4):
                js = slice(c * 512 + j * 128, c * 512 + (j + 1) * 128)
                t_z = mm(pz[:, j * 8:(j + 1) * 8], [(QP[:, g, js], zb[g][:, :])], [kvt["b"], q_t[c, g]], z_free)
            t_rz = V.do(lambda e: e.tensor_scalar(rz[g][:, :], pz[:, 0:32], 1e-6, None, ALU.add), t_z, rz_free[g])
            t_rz = V.do(lambda e: e.reciprocal(rz[g][:, :], rz[g][:, :]), t_rz)
            t_rb = A.do(lambda e: e.activation(rb[g][:, :].rearrange("p (h o) -> p h o", o=16),
                                               rz[g][:, :].rearrange("p (h o) -> p h o", o=1).broadcast_to([128, 32, 16]), ACT.Copy), t_rz, rb_free[g])
            rz_free[g] = t_rb
            pn, free, ni = ps.next()
            t_n = mm(pn, [(kvb[g][:, :], QP[:, g, sl])], [], free)
            kvt["at"][g] = t_n
            t_nc = A.do(lambda e: e.activation(zs[g][:, :], pn, ACT.Copy), t_n, zs_free[g])
            ps.free[ni] = t_nc
            return pz, zi, t_rb, t_nc

        def att_m(g, pz, zi, t_rb, t_nc):
            for j in range(4):
                t_b = mm(pz[:, j * 128:(j + 1) * 128], [(rb[g][:, j * 128:(j + 1) * 128], IDN[:, :])], [t_rb])
            rb_free[g] = t_b
            t_a = V.do(lambda e: e.tensor_tensor(at[:, g, :], zs[g][:, :], pz, ALU.mult), t_b, t_nc, kvt["at_v"])
            ps.free[zi] = t_a
            zs_free[g] = t_a
            return t_a

        def att_s(t_a):
            t_h = A.do(lambda e: e.activation(AH[:, :, :], at[:, :, :], ACT.Copy), t_a, kvt["oj"])
            t_l = G.do(lambda e: e.tensor_tensor(AL[:, :, :], at[:, :, :], r32(AH[:, :, :]), ALU.subtract), t_h)
            kvt["at_v"] = t_l
            return [t_h, t_l]

        def att_b(c, m, ts):
            sl = slice(c * 512, (c + 1) * 512)
            p, free, pi = ps.next()
            ms = slice(768 + m * 128, 768 + (m + 1) * 128)
            t_p = mm(p, [x for k in range(2) for x in three(W0H[:, k, ms], W0L[:, k, ms], AH[:, k, :], AL[:, k, :])], ts, free)
            kvt["oj"] = t_p
            t_x[c, m] = V.do(lambda e: e.scalar_tensor_tensor(X[:, m, sl], p, col("ob0", m), X[:, m, sl], ALU.add, ALU.add), t_p, t_x.get((c, m)))
            ps.free[pi] = t_x[c, m]

        def attention0():
            for tt in range(8):
                kv_in(tt)
                yield
                if tt >= 3:
                    kv_out(tt - 3)
                if tt % 4 == 3:
                    for m in range(2):
                        q_unit(tt // 4, m)
                        yield
            for tt in (5, 6, 7):
                kv_out(tt)
            kv_sums()
            yield
            for c in (0, 1):
                parts = att_z(c, 0)
                yield
                att_m(0, *parts)
                parts = att_z(c, 1)
                yield
                ts = att_s(att_m(1, *parts))
                yield
                for tt in range(8 + 4 * c, 12 + 4 * c):
                    kv_in(tt)
                    yield
                    if tt > 10:
                        kv_out(tt - 3)
                for m in range(2):
                    att_b(c, m, ts)
                    yield
            for tt in (13, 14, 15):
                kv_out(tt)
            q_unit(2, 0)
            yield
            kv_sums()
            q_unit(2, 1)
            yield
            for c in (2, 3):
                parts = att_z(c, 0)
                yield
                att_m(0, *parts)
                parts = att_z(c, 1)
                yield
                ts = att_s(att_m(1, *parts))
                yield
                for m in range(2):
                    if c == 2:
                        q_unit(3, m)
                    yield
                yield
                for m in range(2):
                    att_b(c, m, ts)
                    yield

        f_hs = Ring(hh)
        f_sg = Ring(sg)
        bank_free = [None, None]

        def ffn(c, gate_mm, up_mm, tokens, hidden, down, down_tokens, out):
            made = []

            def down_mm(m, sl, th, tl):
                for d in range(2):
                    t = mm(bank[6 + d], down(m, d, hh[sl][:, :], hl[sl][:, :]), [th, tl, *down_tokens],
                           bank_free[d] if m == 0 else None, start=(m == 0), stop=(m == 7))
                f_hs.free[sl] = t
                return t

            for m in range(8):
                pg, free, gi = pf.next()
                t_g = mm(pg, gate_mm(m, c), [*t_xn[c], *tokens], free)
                pu, free, ui = pf.next()
                t_u = mm(pu, up_mm(m, c), [], free)
                s, s_free, si = f_sg.next()
                _, h_free, hi = f_hs.next()
                t_h = hidden(m, s, s_free, pg, t_g, gi, pu, t_u, ui)
                t_hh = A.do(lambda e, s=s, hi=hi: e.activation(hh[hi][:, :], s[:, :], ACT.Copy), t_h, h_free)
                t_hl = G.do(lambda e, s=s, hi=hi: e.tensor_tensor(hl[hi][:, :], s[:, :], r32(hh[hi][:, :]), ALU.subtract), t_hh)
                f_sg.free[si] = t_hl
                made.append((m, hi, t_hh, t_hl))
                if m >= 3:
                    down_mm(*made[m - 3])
                yield
            down_mm(*made[5])
            down_mm(*made[6])
            t = down_mm(*made[7])
            for d in range(2):
                t_x[c, d] = bank_free[d] = out(d, c, t)
            yield

        def hidden0(m, s, s_free, pg, t_g, gi, pu, t_u, ui):
            t_s = A.do(lambda e: e.activation(s[:, :], pg, ACT.Tanh, scale=suh), t_g, s_free, tok["suh"])
            t_s = V.do(lambda e: e.scalar_tensor_tensor(s[:, :], s[:, :], 1.0, pg, ALU.add, ALU.mult), t_s)
            pf.free[gi] = t_s
            t_h = V.do(lambda e: e.tensor_tensor(s[:, :], s[:, :], pu, ALU.mult), t_u, t_s)
            pf.free[ui] = t_h
            return t_h

        def hidden1(m, s, s_free, pg, t_g, gi, pu, t_u, ui):
            t_s = A.do(lambda e: e.activation(s[:, :], pg, ACT.Silu, scale=col("wsg", m)), t_g, s_free)
            pf.free[gi] = t_s
            t_h = V.do(lambda e: e.scalar_tensor_tensor(s[:, :], pu, col("wsu", m), s[:, :], ALU.mult, ALU.mult), t_u, t_s)
            pf.free[ui] = t_h
            return t_h

        def wide(w_h, w_l, m0, c):
            sl = slice(c * 512, (c + 1) * 512)
            ms = slice(m0, m0 + 128)
            if w_l is None:
                return [x for k in range(2) for x in ((w_h[:, k, ms], XH[:, k, sl]), (w_h[:, k, ms], XL[:, k, sl]))]
            return [x for k in range(2) for x in three(w_h[:, k, ms], w_l[:, k, ms], XH[:, k, sl], XL[:, k, sl])]

        def out0(d, c, t):
            sl = slice(c * 512, (c + 1) * 512)
            return V.do(lambda e: e.scalar_tensor_tensor(X[:, d, sl], bank[6 + d], sgd, X[:, d, sl], ALU.mult, ALU.add), t, tok["sgd"], t_x.get((c, d)))

        w1_t, f1_t, fd_t, td_t = [], [], [], []
        done = {}

        def prep_attn1(i, t_w):
            for o, n, H, L in ((0, 768, W1H, W1L), (1536, 256, WOH, WOL)):
                raw = stg[i][:, o:o + 2 * n].rearrange("p (k n) -> p k n", k=2)
                t_h = A.do(lambda e, raw=raw, H=H: e.activation(H[:, :, :], raw, ACT.Copy), t_w, done["att0_pe"])
                t_l = G.do(lambda e, raw=raw, H=H, L=L: e.tensor_tensor(L[:, :, :], raw, r32(H[:, :, :]), ALU.subtract), t_h)
                w1_t.extend([t_h, t_l])
            st_free[i] = t_l

        def prep_ug(n, i, t_w):
            raw = stg[i][:, :].rearrange("p (k n) -> p k n", k=2)
            for k in range(2):
                for h in range(2):
                    p, free, pi = ps.next()
                    hs = slice(h * 512, (h + 1) * 512)
                    ds = slice(n * 1024 + h * 512, n * 1024 + (h + 1) * 512)
                    t_p = mm(p, [(HAD[:, :], raw[:, 0, hs]), ((HADN if k else HAD)[:, :], raw[:, 1, hs])], [t_w, t_hadn], free)
                    t_h = A.do(lambda e, p=p, k=k, ds=ds: e.activation(UGH[:, k, ds], p, ACT.Copy, scale=s16[:, 8 + k:9 + k]), t_p, t_sus, *done["att0"])
                    t_l = V.do(lambda e, p=p, k=k, ds=ds: e.scalar_tensor_tensor(UGL[:, k, ds], p, s16[:, 8 + k:9 + k], r32(UGH[:, k, ds]), ALU.mult, ALU.subtract), t_h)
                    ps.free[pi] = t_l
                    yield
            st_free[i] = t_p
            f1_t.extend([t_h, t_l])

        def butterflies(i, t_w):
            a, bf = stg[i][:, :], stg2
            t = t_w
            for s in (1, 2, 4):
                av, bv = (z.rearrange("p (o t i) -> p o t i", t=2, i=256 * s) for z in (a, bf))
                t = G.do(lambda e, av=av, bv=bv: e.tensor_tensor(bv[:, :, 0, :], av[:, :, 0, :], av[:, :, 1, :], ALU.add), t)
                yield
                t = G.do(lambda e, av=av, bv=bv: e.tensor_tensor(bv[:, :, 1, :], av[:, :, 0, :], av[:, :, 1, :], ALU.subtract))
                yield
                a, bf = bf, a
            st_free[i] = t
            tok["bf"] = t

        def prep_down():
            a, t = stg2, tok["bf"]
            for q in range(4):
                p, free, pi = ps.next()
                t_p = mm(p, [(HAD[:, :], a[:, q * 512:(q + 1) * 512])], [t, t_const], free)
                parts = [(2 * q + r, p[:, r * 256:(r + 1) * 256], s16b[:, 2 * q + r:2 * q + r + 1]) for r in range(2)]
                for cc, pr, sc in parts:
                    t_h = A.do(lambda e, cc=cc, pr=pr, sc=sc: e.activation(DH[:, cc, :], pr, ACT.Copy, scale=sc), t_p, t_sus, *done["att0"])
                for cc, pr, sc in parts:
                    t_l = V.do(lambda e, cc=cc, pr=pr, sc=sc: e.scalar_tensor_tensor(DL[:, cc, :], pr, sc, r32(DH[:, cc, :]), ALU.mult, ALU.subtract), t_h)
                ps.free[pi] = t_l
                yield
            ln_free[0] = ln_free[1] = t_p
            fd_t.extend([t_h, t_l])

        s16b = sb("s16b", 27.75, [128, 8])
        t_sus = V.do(lambda e: e.tensor_scalar(s16[:, 8:10], cols[:, COLS["suu"][0]:COLS["suu"][0] + 2], 1.0 / 16, None, ALU.mult), t_cols, t_const)
        t_sus = V.do(lambda e: e.tensor_scalar(s16b[:, :], cols[:, COLS["sud"][0]:COLS["sud"][0] + 8], 1.0 / 32, None, ALU.mult))
        t_hadn = V.do(lambda e: e.tensor_scalar(HADN[:, :], HAD[:, :], -1.0, None, ALU.mult))

        def ln1(c):
            return layernorm(c, [t_x[c, 0], t_x[c, 1]], T.last, c % 2, (c % 2) * 2, c % 2, ps)

        def ln1_pair(a, b):
            la, lb = ln1(a), ln1(b)
            next(la)
            yield
            next(lb)
            yield
            next(la)
            next(lb)
            yield
            yield
            next(la)
            yield
            next(lb)
            yield

        def scales():
            t = V.do(lambda e: e.tensor_tensor(sgd, sgt, sdn, ALU.mult), tern_t[2])
            t = V.do(lambda e: e.tensor_tensor(sgd, sgd, su, ALU.mult), t)
            tok["sgd"] = V.do(lambda e: e.tensor_scalar(sgd, sgd, 0.5, None, ALU.mult), t)

        def side0():
            for n, _ in enumerate(attention0()):
                if 15 <= n < 18:
                    next(tn)
                    if n == 17:
                        td_t.append(tern_t[2])
                        scales()
                        i, _ = stage(wa1, 1536)
                        loads.append((i, d_st[i].start(S, stg[i][:, 1536:2048], wo1)))
                if n == 18:
                    bf = butterflies(*loads[0])
                if n >= 18 and n % 3 == 1 and "bf" not in tok:
                    next(bf, None)
                    if "bf" in tok:
                        tok["ug0"] = stage(wf1[0], 2048)
                yield
            done["att0_pe"] = T.last()
            done["att0"] = [T.last(), V.last(), A.last(), G.last()]
            prep_attn1(*loads[1])
            ug1 = stage(wf1[1], 2048)
            yield
            yield from prep_down()
            yield from prep_ug(0, *tok["ug0"])
            yield from prep_ug(1, *ug1)
            yield from ln1_pair(0, 1)

        def main0():
            for c in range(NCH):
                yield from ffn(c, lambda m, c: wide(TU, None, m * 128, c), lambda m, c: wide(TG, None, m * 128, c),
                               [tern_t[0], tern_t[1]], hidden0,
                               lambda m, d, h, l: [(TD[:, m, d * 128:(d + 1) * 128], h), (TD[:, m, d * 128:(d + 1) * 128], l)],
                               td_t, out0)

        sd0 = side0()
        next(sd0)
        next(ln0[2])
        next(tn)
        next(sd0)
        next(ln0[3])
        for n in range(FIRST):
            if n < 8:
                next(tn)
            next(sd0)
        tok["suh"] = V.do(lambda e: e.tensor_scalar(suh, su, 0.5, None, ALU.mult), tern_t[0])
        loads = [stage(wf1[2], 2048)]
        d_cs, d_pad = dsem("d_cs"), dsem("d_pad")
        for t, d in ((COS, cos_d), (SIN, sin_d)):
            t_cs = d_cs.start(S, t[:, :], d)
        t_pad = d_pad.start(S, scr_q[:, 48:64, :], pad_d[0:1].broadcast_to([16, 16, NT]))
        t_pad = d_pad.start(S, scr_k[:, 48:64, :], pad_d[1:2].broadcast_to([16, 16, NT]))
        for q in (A, V, G):
            q.wait(*[t for c in range(NCH) for t in t_xn[c]])
        weave(main0(), sd0, RATE0)
        run(sd0)
        t_ffn0_pe = T.last()
        t_ffn0_all = [T.last(), V.last(), A.last(), G.last()]

        rot_free = [None] * 4
        spl_free = [None] * 4
        d_sp = [dsem(f"d_sp{i}") for i in range(4)]

        def qk_unit(c, n):
            sl = slice(c * 512, (c + 1) * 512)
            cs = slice((c % 2) * 512, (c % 2 + 1) * 512)
            name, sc = ("qb1", 0.25) if n == 0 else ("kb1", 1.0)
            pp = []
            for m in range(2):
                p, free, pi = ps.next()
                pp.append((p, pi, mm(p, wide(W1H, W1L, n * 256 + m * 128, c), [*t_xn[c], *w1_t], free)))
            for m, (p, pi, t_p) in enumerate(pp):
                V.do(lambda e, p=p, m=m: e.scalar_tensor_tensor(rot[m][:, :], p, col(name, m), COS[:, cs], ALU.add, ALU.mult),
                     t_p, t_cs, rot_free[m], *t_ffn0_all)
                t = V.do(lambda e, p=p, m=m: e.scalar_tensor_tensor(rot[2 + m][:, :], p, col(name, m), SIN[:, cs], ALU.add, ALU.mult),
                         rot_free[3 - m], rot_free[2 + m])
                ps.free[pi] = t
            t_r = [G.do(lambda e: e.tensor_tensor(rot[0][:, :], rot[0][:, :], rot[3][:, :], ALU.subtract), t),
                   G.do(lambda e: e.tensor_tensor(rot[1][:, :], rot[1][:, :], rot[2][:, :], ALU.add))]
            rot_free[2] = rot_free[3] = t_r[1]
            for m in range(2):
                sh, sl_ = spl[2 * m], spl[2 * m + 1]
                t_h = A.do(lambda e, m=m, sh=sh: e.activation(sh[:, :], rot[m][:, :], ACT.Copy, scale=sc), t_r[m], spl_free[2 * m])
                t_l = V.do(lambda e, m=m, sh=sh, sl_=sl_: e.scalar_tensor_tensor(sl_[:, :], rot[m][:, :], sc, r32(sh[:, :]), ALU.mult, ALU.subtract),
                           t_h, spl_free[2 * m + 1])
                rot_free[m] = t_l
                dst = scr_q if n == 0 else scr_k
                for r in (0, 16 if n == 0 else 32):
                    spl_free[2 * m] = d_sp[2 * m].start(S, dst[:, r + 8 * m:r + 8 * m + 8, sl], sh[:, :], t_h)
                r = 32 if n == 0 else 16
                spl_free[2 * m + 1] = d_sp[2 * m + 1].start(S, dst[:, r + 8 * m:r + 8 * m + 8, sl], sl_[:, :], t_l)

        def v_unit(tt):
            tk = slice(tt * 128, (tt + 1) * 128)
            p, free, pi = ps.next()
            t_p = mm(p[:, 0:256], [x for k in range(2) for x in ((XH[:, k, tk], W1H[:, k, 512:768]), (XH[:, k, tk], W1L[:, k, 512:768]),
                                                                 (XL[:, k, tk], W1H[:, k, 512:768]))], [*t_xn[tt // 4]], free)
            ps.free[pi] = A.do(lambda e: e.activation(VV[:, tt, :, 0:16], p[:, 0:256].rearrange("p (h d) -> p h d", h=16), ACT.Copy), t_p, done["vv"])

        def out1(d, c, t):
            sl = slice(c * 512, (c + 1) * 512)
            return V.do(lambda e: e.scalar_tensor_tensor(X[:, d, sl], bank[6 + d], col("wsd", d), X[:, d, sl], ALU.mult, ALU.add), t)

        d_ks = [dsem(f"d_ks{i}") for i in range(3)]
        d_qs = [dsem(f"d_qs{i}") for i in range(4)]
        d_m = [dsem(f"d_m{i}") for i in range(2)]
        t_ki = [None] * 3
        t_qi = [None] * 4

        def init_slot(i, *tokens):
            for h in range(2):
                t_ki[i] = G.fill(r32(KS[i][h][64 - 64 * h:128 - 64 * h, :]), 0.0, *tokens)

        k_tok = [None] * 16
        q_tok = [None] * 16

        def load(p, *tokens):
            b, j = divmod(p, 8)
            ts = slice(b * 1024, (b + 1) * 1024)
            S.wait(*spl_free, t_pad, *tokens)
            q_tok[p] = d_qs[p % 4].start(S, QS[p % 4][:, :], scr_q[2 * j:2 * j + 2, :, ts])
            for h in range(2):
                k_tok[p] = d_ks[p % 3].start(S, KS[p % 3][h][64 * h:64 * h + 64, :], scr_k[2 * j + h, :, ts])

        NP, LEAD, LAG = 16, 11, 2
        def main1():
            for c in range(NCH):
                yield from ffn(c, lambda m, c: wide(UGH, UGL, 1024 + m * 128, c), lambda m, c: wide(UGH, UGL, m * 128, c), f1_t, hidden1,
                               lambda m, d, h, l: [(DH[:, m, d * 128:(d + 1) * 128], h), (DH[:, m, d * 128:(d + 1) * 128], l),
                                                   (DL[:, m, d * 128:(d + 1) * 128], h)], fd_t, out1)

        def side1():
            init_slot(0, *t_ffn0_all)
            yield from ln1_pair(2, 3)
            for c in (0, 1):
                for n in range(2):
                    qk_unit(c, n)
                    yield
                    j = 8 * c + 4 * n
                    done["vv"] = G.do(lambda e, j=j: e.memset(VV[:, j:j + 4, :, 16:32], 1.0), *t_ffn0_all, *t_xn[3], *fd_t)
                    yield
            load(0, t_ffn0_all[0], *t_ffn0_all, *t_xn[3])
            tiles, tts = iter(range(16)), iter(range(16))

            def tile():
                t_pe[0] = max_tile(0, next(tiles), ps)

            for _ in range(4):
                v_unit(next(tts))
                yield
            for c in (2, 3):
                for n in range(2):
                    qk_unit(c, n)
                    yield
                    v_unit(next(tts))
                    yield
                    tile()
                    yield
                    v_unit(next(tts))
                    yield
                    tile()
                    yield
            for _ in range(4):
                v_unit(next(tts))
                yield
                tile()
                yield
            done["v_pe"], done["v_act"] = T.last(), A.last()
            init_slot(1, V.last())
            load(1, done["v_pe"], V.last(), G.last())
            load(2, *rot_free)
            for n in range(4):
                tile()
                if n == 2:
                    init_slot(2, V.last(), *rot_free)
                yield
            max_rows(0, t_pe[0], ps)
            yield
            for ms in range(8, LEAD):
                for q in range(2):
                    t_pe[1] = max_tile(1, 2 * (ms % 8) + q, ps)
                    yield

        ST = Ring([4, 5, 6])
        mx_free = [None] * 2
        mrow_free = [None] * 2
        pv_free = None
        max_tok = [None] * NP
        m_tok = [None] * NP
        st_last = [None] * NP
        p_tok = {}
        p_free = [None] * 4
        oe_free = [None, None]
        t_pe = [None] * NP

        def max_tile(p, u, both=None):
            h, qt = divmod(u, 8)
            if both:
                if both.i == 1:
                    both.next()
                got = [both.next() for _ in range(2)]
                free, own = [g[1] for g in got], [g[2] for g in got]
                pb = PS[:, own[0]:own[0] + 2, :]
            else:
                i, free, mi = MX.next()
                free = [free]
                pb = PS[:, i:i + 2, :]
            T.wait(*free, k_tok[p], q_tok[p], t_ki[p % 3])
            for half in range(2):
                f = lambda e, half=half: e.matmul(pb[:, half, :], QS[p % 4][:, qt * 128:(qt + 1) * 128],
                                                  KS[p % 3][h][:, half * 512:(half + 1) * 512], start=True, stop=True)
                if half == 0:
                    T.put(f)
                else:
                    t = T.do(f)
            max_tok[p] = V.do(lambda e: e.tensor_reduce(mx[p % 2][:, u:u + 1], pb, AX.XY, ALU.max), t,
                               mx_free[p % 2] if u == 0 else None)
            if both:
                for i in own:
                    both.free[i] = max_tok[p]
            else:
                MX.free[mi] = max_tok[p]
            return t

        def max_rows(p, t_pe, ring):
            o, free, si = ring.next()
            if ring is ST:
                o = bank[o]
            t = T.do(lambda e: e.transpose(o[0:16, 0:128], mx[p % 2][:, :], IDN[:, :]), free, max_tok[p])
            mx_free[p % 2] = t
            t = A.do(lambda e: e.activation(mrow[p % 2][:, :], o[0:16, 0:128], ACT.Copy, scale=-1.0), t, mrow_free[p % 2])
            ring.free[si] = t
            m_tok[p] = d_m[p % 2].start(S, QS[p % 4][48:113:64, :].rearrange("a (q n) -> a q n", q=8), mrow[p % 2][:, :], t, t_pe)
            mrow_free[p % 2] = m_tok[p]

        def scores(s, c):
            p, kt = divmod(s, 8)
            h, half = divmod(c, 2)
            i, free, si = ST.next()
            t = T.do(lambda e: e.matmul(PS[:, i, :], KS[p % 3][h][:, kt * 128:(kt + 1) * 128], QS[p % 4][:, half * 512:(half + 1) * 512],
                                        start=True, stop=True), free, m_tok[p])
            st_last[p] = t
            ST.free[si] = A.do(lambda e: e.activation(P[s % 4][:, c * 512:(c + 1) * 512], PS[:, i, :], ACT.Exp), t, p_free[s % 4] if c == 0 else None)
            p_tok[s] = ST.free[si]

        def values(s):
            nonlocal pv_free
            p, kt = divmod(s, 8)
            b, j = divmod(p, 8)
            T.wait(p_tok[s], done["v_act"], pv_free if kt == 0 else None)
            for c in range(4):
                f = lambda e, c=c: e.matmul(PS[32 * c:32 * c + 32, 7, :], VV[:, 8 * b + kt, 2 * j + c // 2, :], P[s % 4][:, c * 512:(c + 1) * 512],
                                            start=(kt == 0), stop=(kt == 7), tile_position=(0, 32 * c))
                if c < 3:
                    T.put(f)
                else:
                    t = T.do(f)
            p_free[s % 4] = t
            if p == NP - 1 and kt == 7:
                last_pair(t)
            elif kt == 7:
                o = p % 2
                g = p // 4
                pv_free = A.do(lambda e: e.activation(OE[o][:, :], PS[:, 7, :], ACT.Copy), t, oe_free[o])
                dq, s_o, s_n, s_r, _ = ways(p)
                t_w = s_o.start(dq, scr_o[p].rearrange("c k n -> (c k) n"), OE[o][:, :], pv_free)
                oe_free[o] = t_w
                t = s_r.start(dq, RC[o][:, :], scr_o[p, :, 16, :].rearrange("c (q n) -> c q n", n=16), t_w, rc_free[o])
                for h in range(2):
                    row = 32 * (p % 4) + 16 * h
                    s_n.start(dq, NUM[g % 2][row:row + 16, :].rearrange("r (a n) -> r a n", a=2),
                                       scr_o[p, 2 * h:2 * h + 2, 0:16, :].rearrange("a r n -> r a n"), t_w, num_free[g % 2], t_ffn1_pe)
                later(now[0] + (4 if p < NP - 2 else 1), lambda: recip(p, t))
                if p == 12:
                    G.fill(NUM[1][96:128, :], 0.0, num_free[1])
                    t_fill.append(G.fill(DEN[1][96:128, :], 1.0))

        def last_pair(t_pv):
            oe, b = OE[1], NP // 8 - 1
            halves = [slice(0, 256), slice(256, 512)]
            t_o = [A.do(lambda e, qs=qs: e.activation(oe[:, qs], PS[:, 7, qs], ACT.Copy), t_pv, oe_free[1]) for qs in halves]
            den = []
            for qs, t in zip(halves, t_o):
                k, free, si = ST.next()
                den.append((k, si, mm(PS[:, k, 0:256], [(SEL[:, :], oe[:, qs])], [t, *t_last], free)))
            acc = []
            for cc in range(2):
                for m in range(2):
                    k, free, si = ST.next()
                    acc.append((cc, m, k))
                    ms, hs = slice(m * 128, (m + 1) * 128), slice(cc * 512, (cc + 1) * 512)
                    mm(PS[:, k, :], three(WOH[:, 1, ms], WOL[:, 1, ms], OH[1][:, hs], OL[1][:, hs]), tok["g3"], free, stop=False)
            parts = []
            for qs, (k, si, t_d) in zip(halves, den):
                t_r = V.do(lambda e, qs=qs, k=k: e.reciprocal(OE[0][:, qs], PS[:, k, 0:256]), t_d, oe_free[0])
                t_n = V.do(lambda e, qs=qs: e.tensor_tensor(OE[0][:, qs], oe[:, qs], OE[0][:, qs], ALU.mult), t_r)
                t_h = A.do(lambda e, qs=qs: e.activation(LH[:, qs], OE[0][:, qs], ACT.Copy), t_n)
                t_l = V.do(lambda e, qs=qs: e.tensor_tensor(LL[:, qs], OE[0][:, qs], r32(LH[:, qs]), ALU.subtract), t_h)
                parts.append([t_h, t_l])
            for q, qs in enumerate(halves):
                for cc, m, k in acc:
                    ms = slice(m * 128, (m + 1) * 128)
                    t_p = mm(PS[:, k, qs], three(WLH[:, cc, ms], WLL[:, cc, ms], LH[:, qs], LL[:, qs]), parts[q], start=False, stop=q == 1)
                    if q == 1:
                        sl = slice((2 * b + cc) * 512, (2 * b + cc + 1) * 512)
                        t_y = V.do(lambda e, k=k, m=m, sl=sl: e.tensor_tensor(X[:, m, sl], PS[:, k, :], X[:, m, sl], ALU.add), t_p)
                        d_y.start(S, yT[:, m, sl], X[:, m, sl], t_y)

        def recip(p, t_in):
            o, g = p % 2, p // 4
            t = V.do(lambda e: e.reciprocal(RC[o][:, :], RC[o][:, :]), t_in)
            dq, _, s_n, _, s_s = ways(p)
            t = s_s.start(dq, scr_r[p].rearrange("c (q n) -> (c q) n", n=16), RC[o][:, :], t)
            rc_free[o] = t
            for h in range(2):
                row = 32 * (p % 4) + 16 * h
                s_n.start(dq, DEN[g % 2][row:row + 16, :].rearrange("r (a n) -> r a n", a=2),
                                   scr_r[p, 2 * h:2 * h + 2, :].rearrange("(o a) n -> o a n", o=1).broadcast_to([16, 2, 512]), t, num_free[g % 2])
            if p % 4 == 3 or p == NP - 2:
                later(now[0] + (4 if g < 3 else 1), lambda: group(g))

        def group(g):
            i = g % 2
            b, f = divmod(g, 2)
            t_n = (G if g < 3 else V).do(lambda e: e.tensor_tensor(NUM[i][:, :], NUM[i][:, :], DEN[i][:, :], ALU.mult),
                                         (d_num[i].sem, d_num[i].n), *([(d_late[1].sem, d_late[1].n), *t_fill] if g == 3 else []))
            if g < 3:
                t_h = A.do(lambda e: e.activation(OH[i][:, :], NUM[i][:, :], ACT.Identity, bias=col("vb1", f)), t_n, oh_free[i])
            else:
                t_h = V.do(lambda e: e.tensor_scalar(OH[i][:, :], NUM[i][:, :], col("vb1", f), None, ALU.add), t_n, oh_free[i])
            t_l = V.do(lambda e: e.scalar_tensor_tensor(OL[i][:, :], NUM[i][:, :], col("vb1", f), r32(OH[i][:, :]), ALU.add, ALU.subtract), t_h)
            num_free[i] = t_l
            if g == 3:
                tok["g3"] = [t_h, t_l]
                return
            for n in range(4):
                later(now[0] + 1 + n, lambda n=n: project(g, n, [t_h, t_l]))

        def project(g, n, ts):
            i = g % 2
            b, f = divmod(g, 2)
            cc, m = divmod(n, 2)
            hs = slice(cc * 512, (cc + 1) * 512)
            sl = slice((2 * b + cc) * 512, (2 * b + cc + 1) * 512)
            ms = slice(m * 128, (m + 1) * 128)
            k, free, si = ST.next()
            t_p = mm(PS[:, k, :], three(WOH[:, f, ms], WOL[:, f, ms], OH[i][:, hs], OL[i][:, hs]), ts, free)
            oh_free[i] = t_p
            if f == 0:
                t_o = V.do(lambda e: e.scalar_tensor_tensor(X[:, m, sl], PS[:, k, :], col("ob1", m), X[:, m, sl], ALU.add, ALU.add), t_p)
            else:
                t_o = V.do(lambda e: e.tensor_tensor(X[:, m, sl], PS[:, k, :], X[:, m, sl], ALU.add), t_p, t_x[2 * b + cc, m])
            t_x[2 * b + cc, m] = t_o
            ST.free[si] = t_o
            if g == 1:
                d_y.start(S, yT[:, m, sl], X[:, m, sl], t_o)

        d_y = dsem("d_y")
        t_fill = []
        d_late = [dsem(f"d_late{i}") for i in range(4)]

        def ways(p):
            if p == NP - 2:
                return (S, *d_late)
            return G, d_oe[p % 2], d_num[p // 4 % 2], d_rc[p % 2], d_rs[p % 2]

        d_oe = [dsem(f"d_oo{i}") for i in range(2)]
        d_num = [dsem(f"d_num{i}") for i in range(2)]
        d_rc = [dsem(f"d_rc{i}") for i in range(2)]
        d_rs = [dsem(f"d_rs{i}") for i in range(2)]
        num_free, rc_free, oh_free = [None] * 2, [None] * 2, [None] * 2
        plan = {}
        now = [0]

        def later(s, f):
            plan.setdefault(s, []).append(f)

        s_free = ps.free
        ps = Ring(bank[0:3])
        ps.free = [*s_free, kvt["kv_free"]]
        sd1 = side1()
        weave(main1(), sd1, RATE1)
        run(sd1)
        t_ffn1_pe = T.last()
        t_end = [V.last(), A.last()]
        MX = Ring([0, 2])
        MX.free = [V.last(), V.last()]
        ST.free = [V.last()] * 3
        T.wait(*t_end, G.last())
        for q in (A, V):
            q.wait(t_ffn1_pe)
        A.wait(V.last(), G.last())
        G.wait(t_ffn1_pe)
        d_wl = dsem("d_wl")
        d_wl.start(S, SEL[:, :], sel_d, t_ffn1_pe, t_end[1])
        t_wl = d_wl.start(S, WLR[:, :, :], wl_d)
        t_h = G.do(lambda e: e.tensor_copy(WLH[:, :, :], WLR[:, :, :]), t_wl)
        t_last = [t_wl, G.do(lambda e: e.tensor_tensor(WLL[:, :, :], WLR[:, :, :], r32(WLH[:, :, :]), ALU.subtract), t_h)]
        MR = 0
        s = 0
        while s < 8 * NP + LAG or any(k >= s for k in plan):
            now[0] = s
            ms = s + LEAD
            live = s < 8 * NP
            maxing = ms < 8 * NP
            if ms == 8 * NP:
                ST.slots += [0, 1, 2, 3]
                ST.free += [x for x in MX.free for _ in range(2)]
            for f in plan.get(s, []):
                f()
            for q in range(2):
                if live:
                    scores(s, 2 * q)
                if maxing:
                    t_pe[ms // 8] = max_tile(ms // 8, 2 * (ms % 8) + q)
                if live:
                    scores(s, 2 * q + 1)
            if 2 <= (ms + MR) // 8 <= NP and (ms + MR) % 8 == 0:
                max_rows((ms + MR) // 8 - 1, t_pe[(ms + MR) // 8 - 1], ST)
            if 0 <= s - LAG < 8 * NP:
                values(s - LAG)
            if live and s % 8 == 7 and s // 8 + 3 < NP:
                load(s // 8 + 3, st_last[s // 8])
            s += 1
        S.wait((d_y.sem, d_y.n))

        block = ctx.enter_context(nc.Block())

        @block.sync
        def _(e):
            S.run(e)

        @block.scalar
        def _(e):
            A.run(e)

        @block.vector
        def _(e):
            V.run(e)

        @block.gpsimd
        def _(e):
            G.run(e)

        @block.tensor
        def _(e):
            T.run(e)


def hadamard(n):
    import numpy as np
    h = np.ones((1, 1), np.float32)
    while h.shape[0] < n:
        h = np.block([[h, h], [h, -h]])
    return np.ascontiguousarray(h, np.float32)


def kernel(**inp):
    import numpy as np
    import concourse.bacc as bacc
    from concourse.bass_utils import run_bass_kernel_spmd as run

    inp = {k: np.asarray(v) for k, v in inp.items()}

    def fold(w):
        n, d = w.shape
        return w.T.reshape(d // 128, 128, n).transpose(1, 0, 2)

    def flat(w):
        return np.ascontiguousarray(w.reshape(128, -1))

    half = np.arange(256).reshape(16, 2, 8).transpose(1, 0, 2).reshape(-1)
    x = inp["L0_attn_hidden_states"]
    xT = np.ascontiguousarray(fold(x.reshape(NT, 256)))
    wa0 = flat(np.concatenate([fold(inp[f"L0_attn_{n}_w"]) for n in "qkvo"], axis=2))
    tern = [flat(fold(inp[f"L0_ffn_W_{n}"])) for n in ("up", "gate", "down")]
    q, k, v = (inp[f"L1_attn_{n}_w"] for n in "qkv")
    wa1 = flat(fold(np.concatenate([q[half], k[half], v], axis=0)))
    wo1 = flat(fold(inp["L1_attn_out_w"]))
    wf1 = [flat(fold(inp[f"L1_ffn_W_{n}"])) for n in ("up", "gate", "down")]

    def cut(a):
        return a.reshape(-1, 128).T

    qb, kb = inp["L1_attn_q_b"], inp["L1_attn_k_b"]
    ws = inp["L1_ffn_Wscale_ug"]
    part = np.arange(128)
    cols = np.ascontiguousarray(np.concatenate([
        cut(inp["L0_attn_q_b"]), cut(inp["L0_attn_o_b"]), cut(qb[half]), cut(qb[half]), cut(kb[half]), cut(kb[half]),
        cut(inp["L1_attn_v_b"]), cut(inp["L1_attn_out_b"]), cut(inp["L1_ffn_SU_ug"]), cut(inp["L1_ffn_SU_dp"]),
        cut(ws[:1024]), cut(ws[1024:]), cut(inp["L1_ffn_Wscale_dp"]),
        (part == 48).astype(np.float32)[:, None], (part == 112).astype(np.float32)[:, None],
        np.full((128, 1), 1e-6, np.float32), np.full((128, 1), 1e-5, np.float32)], axis=1))
    bkv = np.ascontiguousarray(np.broadcast_to(np.concatenate([inp["L0_attn_k_b"], inp["L0_attn_v_b"]])[None, :], (128, 512)))
    inv = (1.0 / np.float32(10000.0) ** (np.arange(0, 16, 2, dtype=np.float32) / np.float32(16))).astype(np.float32)
    fr = np.arange(1024, dtype=np.float32)[:, None] * inv[None, :]
    cos = np.ascontiguousarray(np.tile(np.cos(fr).T, (16, 1)).astype(np.float32))
    sin = np.ascontiguousarray(np.tile(np.sin(fr).T, (16, 1)).astype(np.float32))
    mask = (part[:, None] // 16 == part[None, :] // 16).astype(np.float32)
    arrays = dict(xT=xT, wa0=wa0, wa1=wa1, wo1=wo1, cols=cols, bkv=bkv, cos=cos, sin=sin, had=hadamard(128),
                  mask=mask, ident=np.eye(128, dtype=np.float32))
    wl = np.zeros((128, 2, 256), np.float32)
    sel = np.zeros((128, 128), np.float32)
    sel[part // 32 * 32 + 16, part] = 1.0
    wo = fold(inp["L1_attn_out_w"])
    for c in range(4):
        h, half = divmod(c, 2)
        wl[32 * c:32 * c + 16, half] = wo[96 + 16 * h:112 + 16 * h, 1]
    arrays["sel"], arrays["wl"] = sel, wl
    pad = np.zeros((2, 16, NT), np.float32)
    pad[1, 0] = 1.0
    arrays["pad"] = pad
    for i in range(3):
        arrays[f"tern{i}"] = tern[i]
        arrays[f"wf1{i}"] = wf1[i]
    arrays = {f"in_{n}": a for n, a in arrays.items()}

    nc = bacc.Bacc("TRN2", target_bir_lowering=False, num_devices=1)
    t = {n: nc.dram_tensor(n, a.shape, F32, kind="ExternalInput").ap() for n, a in arrays.items()}
    y = nc.dram_tensor("out_y", (128, 2, NT), F32, kind="ExternalOutput").ap()
    program(nc, t["in_xT"], t["in_wa0"], [t[f"in_tern{i}"] for i in range(3)], t["in_wa1"], t["in_wo1"],
            [t[f"in_wf1{i}"] for i in range(3)], t["in_cols"], t["in_bkv"], t["in_cos"], t["in_sin"], t["in_had"], t["in_mask"],
            t["in_ident"], t["in_pad"], t["in_sel"], t["in_wl"], y)
    r = run(nc, [arrays], core_ids=[0])
    out = np.asarray(r.results[0]["out_y"])
    return np.ascontiguousarray(out.transpose(2, 1, 0).reshape(2, 1024, 256))
```
